# Optimizing a Trainium2 kernel written in Bass

```python
import numpy as np
import jax
import jax.numpy as jnp

def _softmax(x, axis=-1):
    return jax.nn.softmax(x, axis=axis)

def _gelu(x):
    return jax.nn.gelu(x, approximate=True)

def _silu(x):
    return jax.nn.silu(x)

def _sigmoid(x):
    return jax.nn.sigmoid(x)

def _layernorm(x, axis=-1, eps=1e-05):
    m = jnp.mean(x, axis=axis, keepdims=True)
    v = jnp.var(x, axis=axis, keepdims=True)
    return (x - m) / jnp.sqrt(v + eps)

def _scatter_add(tgt, idx, src, axis=0):
    return tgt.at[idx].add(src)

def _segment_sum(src, seg, n):
    return jax.ops.segment_sum(src, seg, n)
kernel_name = 'mk_dlrm_tower_d1_rec_r8_7b9e46'

def setup_inputs(seed: int=0):
    np.random.seed(seed)
    _w = jnp.asarray

    def _rec_inputs():
        import jax
        import jax.numpy as jnp
        _tk = jax.random.key(seed)
        dense_ctx = jax.random.normal(jax.random.fold_in(_tk, 190), (512, 16), jnp.float32)
        ids = jnp.stack([jax.random.randint(jax.random.fold_in(_tk, 200 + f), (512,), 0, v, jnp.int32) for f, v in enumerate([1000, 12500, 1000, 12500, 12500, 1250, 1250, 12500, 1000, 12500, 12500, 125000, 1250, 12500, 1250, 125000, 12500, 1250, 125000, 12500, 12500, 1250, 12500, 12500, 125000, 12500, 1000, 125000, 1000, 1000, 1250, 125000])], axis=1)
        tbl_0 = 0.05 * jax.random.normal(jax.random.fold_in(_tk, 500 + 0), (1000, 32), jnp.float32)
        tbl_1 = 0.05 * jax.random.normal(jax.random.fold_in(_tk, 500 + 1), (12500, 32), jnp.float32)
        tbl_2 = 0.05 * jax.random.normal(jax.random.fold_in(_tk, 500 + 2), (1000, 32), jnp.float32)
        tbl_3 = 0.05 * jax.random.normal(jax.random.fold_in(_tk, 500 + 3), (12500, 32), jnp.float32)
        tbl_4 = 0.05 * jax.random.normal(jax.random.fold_in(_tk, 500 + 4), (12500, 32), jnp.float32)
        tbl_5 = 0.05 * jax.random.normal(jax.random.fold_in(_tk, 500 + 5), (1250, 32), jnp.float32)
        tbl_6 = 0.05 * jax.random.normal(jax.random.fold_in(_tk, 500 + 6), (1250, 32), jnp.float32)
        tbl_7 = 0.05 * jax.random.normal(jax.random.fold_in(_tk, 500 + 7), (12500, 32), jnp.float32)
        tbl_8 = 0.05 * jax.random.normal(jax.random.fold_in(_tk, 500 + 8), (1000, 32), jnp.float32)
        tbl_9 = 0.05 * jax.random.normal(jax.random.fold_in(_tk, 500 + 9), (12500, 32), jnp.float32)
        tbl_10 = 0.05 * jax.random.normal(jax.random.fold_in(_tk, 500 + 10), (12500, 32), jnp.float32)
        tbl_11 = 0.05 * jax.random.normal(jax.random.fold_in(_tk, 500 + 11), (125000, 32), jnp.float32)
        tbl_12 = 0.05 * jax.random.normal(jax.random.fold_in(_tk, 500 + 12), (1250, 32), jnp.float32)
        tbl_13 = 0.05 * jax.random.normal(jax.random.fold_in(_tk, 500 + 13), (12500, 32), jnp.float32)
        tbl_14 = 0.05 * jax.random.normal(jax.random.fold_in(_tk, 500 + 14), (1250, 32), jnp.float32)
        tbl_15 = 0.05 * jax.random.normal(jax.random.fold_in(_tk, 500 + 15), (125000, 32), jnp.float32)
        tbl_16 = 0.05 * jax.random.normal(jax.random.fold_in(_tk, 500 + 16), (12500, 32), jnp.float32)
        tbl_17 = 0.05 * jax.random.normal(jax.random.fold_in(_tk, 500 + 17), (1250, 32), jnp.float32)
        tbl_18 = 0.05 * jax.random.normal(jax.random.fold_in(_tk, 500 + 18), (125000, 32), jnp.float32)
        tbl_19 = 0.05 * jax.random.normal(jax.random.fold_in(_tk, 500 + 19), (12500, 32), jnp.float32)
        tbl_20 = 0.05 * jax.random.normal(jax.random.fold_in(_tk, 500 + 20), (12500, 32), jnp.float32)
        tbl_21 = 0.05 * jax.random.normal(jax.random.fold_in(_tk, 500 + 21), (1250, 32), jnp.float32)
        tbl_22 = 0.05 * jax.random.normal(jax.random.fold_in(_tk, 500 + 22), (12500, 32), jnp.float32)
        tbl_23 = 0.05 * jax.random.normal(jax.random.fold_in(_tk, 500 + 23), (12500, 32), jnp.float32)
        tbl_24 = 0.05 * jax.random.normal(jax.random.fold_in(_tk, 500 + 24), (125000, 32), jnp.float32)
        tbl_25 = 0.05 * jax.random.normal(jax.random.fold_in(_tk, 500 + 25), (12500, 32), jnp.float32)
        tbl_26 = 0.05 * jax.random.normal(jax.random.fold_in(_tk, 500 + 26), (1000, 32), jnp.float32)
        tbl_27 = 0.05 * jax.random.normal(jax.random.fold_in(_tk, 500 + 27), (125000, 32), jnp.float32)
        tbl_28 = 0.05 * jax.random.normal(jax.random.fold_in(_tk, 500 + 28), (1000, 32), jnp.float32)
        tbl_29 = 0.05 * jax.random.normal(jax.random.fold_in(_tk, 500 + 29), (1000, 32), jnp.float32)
        tbl_30 = 0.05 * jax.random.normal(jax.random.fold_in(_tk, 500 + 30), (1250, 32), jnp.float32)
        tbl_31 = 0.05 * jax.random.normal(jax.random.fold_in(_tk, 500 + 31), (125000, 32), jnp.float32)
        _rk = jax.random.fold_in(_tk, 7)
        W_top1 = 0.0606339 * jax.random.normal(jax.random.fold_in(_tk, 801), (272, 512), jnp.float32)
        W_top2 = 0.0441942 * jax.random.normal(jax.random.fold_in(_tk, 802), (512, 256), jnp.float32)
        W_top3 = 0.0625 * jax.random.normal(jax.random.fold_in(_tk, 803), (256, 1), jnp.float32)
        b_top1 = jnp.zeros((512,), jnp.float32)
        b_top2 = jnp.zeros((256,), jnp.float32)
        return (dense_ctx, ids, tbl_0, tbl_1, tbl_2, tbl_3, tbl_4, tbl_5, tbl_6, tbl_7, tbl_8, tbl_9, tbl_10, tbl_11, tbl_12, tbl_13, tbl_14, tbl_15, tbl_16, tbl_17, tbl_18, tbl_19, tbl_20, tbl_21, tbl_22, tbl_23, tbl_24, tbl_25, tbl_26, tbl_27, tbl_28, tbl_29, tbl_30, tbl_31, W_top1, b_top1, W_top2, b_top2, W_top3)
    dense_ctx, ids, tbl_0, tbl_1, tbl_2, tbl_3, tbl_4, tbl_5, tbl_6, tbl_7, tbl_8, tbl_9, tbl_10, tbl_11, tbl_12, tbl_13, tbl_14, tbl_15, tbl_16, tbl_17, tbl_18, tbl_19, tbl_20, tbl_21, tbl_22, tbl_23, tbl_24, tbl_25, tbl_26, tbl_27, tbl_28, tbl_29, tbl_30, tbl_31, W_top1, b_top1, W_top2, b_top2, W_top3 = _rec_inputs()

    def _L0_rec_setup():
        import jax, jax.numpy as jnp
        import numpy as np
        B, F, D = (512, 32, 32)
        LAYER_SIZE = [128, 128]

        def _cin_forward(inputs, filters):
            x0 = inputs
            prev = inputs
            outs = []
            for W in filters:
                z = jnp.einsum('bhd,bmd->bhmd', x0, prev)
                b, h, m, d = z.shape
                z = z.reshape(b, h * m, d)
                cur = jnp.einsum('bpd,pn->bnd', z, W[0])
                cur = jax.nn.relu(cur)
                prev = cur
                outs.append(cur)
            result = jnp.concatenate(outs, axis=1)
            return jnp.sum(result, axis=-1)
        key = jax.random.key(seed)
        k1, k2, k3 = jax.random.split(key, 3)
        inputs = jax.random.normal(k1, (B, F, D), dtype=jnp.float32)
        field_nums = [F] + LAYER_SIZE
        filter_0 = jax.random.normal(k2, (1, field_nums[0] * field_nums[0], field_nums[1]), dtype=jnp.float32) * 0.05
        filter_1 = jax.random.normal(k3, (1, field_nums[0] * field_nums[1], field_nums[2]), dtype=jnp.float32) * 0.05
        return {'inputs': inputs, 'filter_0': filter_0, 'filter_1': filter_1}
    _L0_rec_all = _L0_rec_setup()
    _L0_rec_in = {k: v for k, v in _L0_rec_all.items() if k in ('filter_0', 'filter_1')}
    del _L0_rec_all
    return {'dense_ctx': dense_ctx, 'ids': ids, 'tbl_0': tbl_0, 'tbl_1': tbl_1, 'tbl_2': tbl_2, 'tbl_3': tbl_3, 'tbl_4': tbl_4, 'tbl_5': tbl_5, 'tbl_6': tbl_6, 'tbl_7': tbl_7, 'tbl_8': tbl_8, 'tbl_9': tbl_9, 'tbl_10': tbl_10, 'tbl_11': tbl_11, 'tbl_12': tbl_12, 'tbl_13': tbl_13, 'tbl_14': tbl_14, 'tbl_15': tbl_15, 'tbl_16': tbl_16, 'tbl_17': tbl_17, 'tbl_18': tbl_18, 'tbl_19': tbl_19, 'tbl_20': tbl_20, 'tbl_21': tbl_21, 'tbl_22': tbl_22, 'tbl_23': tbl_23, 'tbl_24': tbl_24, 'tbl_25': tbl_25, 'tbl_26': tbl_26, 'tbl_27': tbl_27, 'tbl_28': tbl_28, 'tbl_29': tbl_29, 'tbl_30': tbl_30, 'tbl_31': tbl_31, 'W_top1': W_top1, 'b_top1': b_top1, 'W_top2': W_top2, 'b_top2': b_top2, 'W_top3': W_top3, 'L0_rec_filter_0': _L0_rec_in['filter_0'], 'L0_rec_filter_1': _L0_rec_in['filter_1']}

def reference(dense_ctx, ids, tbl_0, tbl_1, tbl_2, tbl_3, tbl_4, tbl_5, tbl_6, tbl_7, tbl_8, tbl_9, tbl_10, tbl_11, tbl_12, tbl_13, tbl_14, tbl_15, tbl_16, tbl_17, tbl_18, tbl_19, tbl_20, tbl_21, tbl_22, tbl_23, tbl_24, tbl_25, tbl_26, tbl_27, tbl_28, tbl_29, tbl_30, tbl_31, W_top1, b_top1, W_top2, b_top2, W_top3, L0_rec_filter_0, L0_rec_filter_1):
    import jax
    import jax.numpy as jnp

    def _L0_rec_ref(inputs, filter_0, filter_1):
        import jax, jax.numpy as jnp
        import numpy as np
        B, F, D = (512, 32, 32)
        LAYER_SIZE = [128, 128]

        def _cin_forward(inputs, filters):
            x0 = inputs
            prev = inputs
            outs = []
            for W in filters:
                z = jnp.einsum('bhd,bmd->bhmd', x0, prev)
                b, h, m, d = z.shape
                z = z.reshape(b, h * m, d)
                cur = jnp.einsum('bpd,pn->bnd', z, W[0])
                cur = jax.nn.relu(cur)
                prev = cur
                outs.append(cur)
            result = jnp.concatenate(outs, axis=1)
            return jnp.sum(result, axis=-1)
        return _cin_forward(inputs, (filter_0, filter_1))
    e = jnp.stack([tbl_0[ids[:, 0]], tbl_1[ids[:, 1]], tbl_2[ids[:, 2]], tbl_3[ids[:, 3]], tbl_4[ids[:, 4]], tbl_5[ids[:, 5]], tbl_6[ids[:, 6]], tbl_7[ids[:, 7]], tbl_8[ids[:, 8]], tbl_9[ids[:, 9]], tbl_10[ids[:, 10]], tbl_11[ids[:, 11]], tbl_12[ids[:, 12]], tbl_13[ids[:, 13]], tbl_14[ids[:, 14]], tbl_15[ids[:, 15]], tbl_16[ids[:, 16]], tbl_17[ids[:, 17]], tbl_18[ids[:, 18]], tbl_19[ids[:, 19]], tbl_20[ids[:, 20]], tbl_21[ids[:, 21]], tbl_22[ids[:, 22]], tbl_23[ids[:, 23]], tbl_24[ids[:, 24]], tbl_25[ids[:, 25]], tbl_26[ids[:, 26]], tbl_27[ids[:, 27]], tbl_28[ids[:, 28]], tbl_29[ids[:, 29]], tbl_30[ids[:, 30]], tbl_31[ids[:, 31]]], axis=1)
    z = _L0_rec_ref(e, L0_rec_filter_0, L0_rec_filter_1)
    z = z.reshape(z.shape[0], -1)
    h = jnp.concatenate([z, dense_ctx], axis=1)
    h = jnp.maximum(h @ W_top1 + b_top1, 0.0)
    h = jnp.maximum(h @ W_top2 + b_top2, 0.0)
    y = h @ W_top3
    return y

_drawn_inputs = setup_inputs


def setup_inputs(seed=0):
    import zlib

    import numpy as np

    out = dict(_drawn_inputs(seed))
    spreads = {'b_top1': (0.0, 0.414), 'b_top2': (0.0, 0.405)}
    factors = {'tbl_0': 5.504,
     'tbl_1': 5.95,
     'tbl_2': 5.927,
     'tbl_3': 5.849,
     'tbl_4': 5.702,
     'tbl_5': 5.907,
     'tbl_6': 5.729,
     'tbl_7': 5.858,
     'tbl_8': 6.246,
     'tbl_9': 6.069,
     'tbl_10': 5.584,
     'tbl_11': 6.148,
     'tbl_12': 5.774,
     'tbl_13': 5.94,
     'tbl_14': 6.143,
     'tbl_15': 5.995,
     'tbl_16': 6.237,
     'tbl_17': 5.65,
     'tbl_18': 6.188,
     'tbl_19': 5.901,
     'tbl_20': 5.926,
     'tbl_21': 6.039,
     'tbl_22': 5.784,
     'tbl_23': 6.188,
     'tbl_24': 6.5,
     'tbl_25': 5.692,
     'tbl_26': 5.854,
     'tbl_27': 6.101,
     'tbl_28': 5.813,
     'tbl_29': 6.082,
     'tbl_30': 6.447,
     'tbl_31': 5.594,
     'L0_rec_filter_1': 8.0}
    for name, (base, spread) in spreads.items():
        noise = np.random.default_rng([zlib.crc32(name.encode()), seed]).standard_normal(out[name].shape)
        drawn = base * np.exp(spread * noise) if base else spread * noise
        out[name] = jnp.asarray(drawn.astype(out[name].dtype))
    for name, factor in factors.items():
        out[name] = (out[name] * factor).astype(out[name].dtype)
    return out
```

```python
from contextlib import ExitStack

import concourse.bass as bass
from concourse import mybir

F32 = mybir.dt.float32
F32R = mybir.dt.float32r
I32 = mybir.dt.int32
ALU = mybir.AluOpType
ACT = mybir.ActivationFunctionType
AXX = mybir.AxisListType.X

P = 128
B, F, D = 512, 32, 32
N1 = N2 = 128
DENSE = 16
H1, H2 = 512, 256
Q = P // F
TD = 4
COLS = TD * P
BLOCKS = B // P
PER_BLOCK = D // TD
NT = BLOCKS * PER_BLOCK
G = F // Q
V = N1 // F
J = 5
RING = 4
AHEAD = 3
K1T = 3

KIND = ["vector", "pool", "plain", "pool", "pool", "vector", "pool", "pool"]


def count(kinds, tile, g):
    return sum(k in kinds for k in KIND) * tile + sum(k in kinds for k in KIND[:g + 1])


def live(tile):
    return not isinstance(tile, int) or 0 <= tile < NT


def due(n):
    return not isinstance(n, int) or n > 0


def tower(nc, a, tables, out):
    with ExitStack() as ctx:
        def sb(name, shape, dt=F32):
            return ctx.enter_context(nc.sbuf_tensor(name, shape, dt))

        def ps(name, shape=(P, COLS)):
            return ctx.enter_context(nc.psum_tensor(name, list(shape), F32))

        def sem(name):
            return ctx.enter_context(nc.semaphore(name))

        ids = sb("ids_sb", [P, BLOCKS, F], I32)
        rows = sb("rows", [P, 2, F, D])
        ident = sb("ident_sb", [P, P])
        sel = sb("sel_r", [2 * F, G + J, P], F32R)
        w1 = sb("w1", [P, J, N1])
        w2_hi = sb("w2_hi", [P, G, V, N2], F32R)
        w2_lo = sb("w2_lo", [P, G, V, N2], F32R)
        plain_steps = [g for g in range(G) if KIND[g] == "plain"]
        w2_plain = sb("w2_plain", [P, max(1, len(plain_steps)), V, N2])
        dense = sb("dense_sb", [DENSE, B])
        bias1 = sb("bias1", [P, H1 // P])
        bias2 = sb("bias2", [P, H2 // P])
        w_top3 = sb("w_top3_sb", [P, H2 // P])
        staged = sb("staged", [P, 2, TD, Q, F])
        x_split = sb("x_split", [2 * F, 2, COLS], F32R)
        x_rep = sb("x_rep", [P, 2, COLS])
        z1 = sb("z1", [P, 2, COLS])
        cur1 = sb("cur1", [P, 2, V, COLS])
        z = sb("z", [P, RING, V, COLS])
        z_hi = sb("z_hi", [P, RING, V, COLS], F32R)
        z_lo = sb("z_lo", [P, RING, V, COLS], F32R)
        sum1 = sb("sum1", [P, BLOCKS, COLS])
        sum2 = sb("sum2", [P, BLOCKS, COLS])
        y_row = sb("y_row", [1, B])

        w2_raw = z[:, 0:2].rearrange("p r v c -> p (r v c)").rearrange("p (g n) -> p g n", g=G)
        sel_raw = z[0:2 * F, 2].rearrange("p v c -> p (v c)")[:, 0:(G + J) * P]
        w1_back = z[:, 3].rearrange("p v c -> p (v c)")[:, 0:J * N1]
        w_top1 = rows[:, :].rearrange("p t f d -> p (t f d)")[:, 0:K1T * H1].rearrange(
            "p (k n) -> p k n", k=K1T)
        sums = cur1[:, 0, 0:2]
        w_top2 = cur1[:, 0, 2:4].rearrange("p v c -> p (v c)").rearrange("p (k n) -> p k n", n=H2)
        hid1 = z[:, 0]
        hid2 = z[:, 1, 0:H2 // P]

        spread = [ps(f"spread{i}") for i in range(2)]
        rolled = [ps(f"rolled{i}") for i in range(2)]
        x_t = ps("x_t")
        acc1 = ps("acc1")
        acc2 = [ps(f"acc2_{i}") for i in range(2)]

        s_ids = sem("s_ids")
        s_ident = sem("s_ident")
        s_sel_in = sem("s_sel_in")
        s_w1_in = sem("s_w1_in")
        s_w2_in = sem("s_w2_in")
        s_plain_in = sem("s_plain_in")
        s_small_in = sem("s_small_in")
        s_top1_in = sem("s_top1_in")
        s_top2_in = sem("s_top2_in")
        s_gather = [sem(f"s_gather{t}") for t in range(BLOCKS)]
        s_out = sem("s_out")
        s_w2_hi = sem("s_w2_hi")
        s_w2_lo = sem("s_w2_lo")
        s_sel = sem("s_sel")
        s_w1 = sem("s_w1")
        s_zeroed = sem("s_zeroed")
        s_rows = sem("s_rows")
        s_staged = sem("s_staged")
        s_x_t = sem("s_x_t")
        s_x_rep = sem("s_x_rep")
        s_x_hi = sem("s_x_hi")
        s_x_lo = sem("s_x_lo")
        s_rolled = sem("s_rolled")
        s_z1 = sem("s_z1")
        s_l1 = sem("s_l1")
        s_sum1 = sem("s_sum1")
        s_cur1 = sem("s_cur1")
        s_spread = sem("s_spread")
        s_z = sem("s_z")
        s_z_hi = sem("s_z_hi")
        s_z_lo_v = sem("s_z_lo_v")
        s_z_lo_p = sem("s_z_lo_p")
        s_l2 = sem("s_l2")
        s_sum2 = sem("s_sum2")
        s_sums = sem("s_sums")
        s_h1 = sem("s_h1")
        s_hid1 = sem("s_hid1")
        s_h2 = sem("s_h2")
        s_hid2 = sem("s_hid2")
        s_y = sem("s_y")
        s_y_row = sem("s_y_row")

        LAST = NT // 2 - 1
        CUR1 = Q * V

        def over_pairs(eng, pair_of_tiles):
            pair_of_tiles(-1)
            pair_of_tiles(0)
            with eng.Fori(1, LAST) as pair:
                pair_of_tiles(pair)
            pair_of_tiles(LAST)

        block = ctx.enter_context(nc.Block())

        @block.sync
        def _(sp):
            sp.dma_start(ids[:], a["ids"]).then_inc(s_ids, 16)
            sp.dma_start(ident[:], a["ident"]).then_inc(s_ident, 16)
            sp.dma_start(sel_raw, a["sel"]).then_inc(s_sel_in, 16)
            sp.dma_start(w1[:].rearrange("p j n -> p (j n)"), a["w1_forth"]).then_inc(s_w1_in, 16)
            sp.dma_start(w1_back, a["w1_back"]).then_inc(s_w1_in, 16)
            sp.dma_start(w2_raw, a["w2"]).then_inc(s_w2_in, 16)
            for n, g in enumerate(plain_steps):
                sp.dma_start(w2_plain[:, n].rearrange("p v n -> p (v n)"), a["w2"][:, g]).then_inc(
                    s_plain_in, 16)
            sp.dma_start(dense[:], a["dense"]).then_inc(s_small_in, 16)
            sp.dma_start(bias1[:], a["b_top1"]).then_inc(s_small_in, 16)
            sp.dma_start(bias2[:], a["b_top2"]).then_inc(s_small_in, 16)
            sp.dma_start(w_top3[:], a["w_top3"]).then_inc(s_small_in, 16)
            sp.wait_ge(s_staged, NT)
            sp.dma_start(w_top1[:, 0:2], a["w_top1"][0:2 * P].rearrange("(k p) n -> p k n", p=P)
                         ).then_inc(s_top1_in, 16)
            sp.dma_start(w_top1[0:DENSE, 2], a["w_top1"][2 * P:]).then_inc(s_top1_in, 16)
            sp.wait_ge(s_z, G * (NT - 1))
            sp.dma_start(w_top2, a["w_top2"].rearrange("(k p) n -> p k n", p=P)).then_inc(
                s_top2_in, 16)
            sp.wait_ge(s_y_row, 1)
            sp.dma_start(out, y_row[:]).then_inc(s_out, 16)
            sp.wait_ge(s_out, 16)

        @block.gpsimd
        def _(pool):
            def gather(t, fields):
                for f in fields:
                    nc.gpsimd.indirect_dma_start(
                        out=rows[:, t % 2, f, :], out_offset=None, in_=tables[f],
                        in_offset=bass.IndirectOffsetOnAxis(ap=ids[:, t, f:f + 1], axis=0),
                    ).then_inc(s_gather[t], 16)

            def gathered(t):
                pool.wait_ge(s_gather[t], 16 * F)
                pool.sem_inc(s_rows, 1)

            def take_rest(tile, g):
                step = G * tile + g
                pool.wait_ge(s_z_hi, count(("pool", "vector"), tile, g))
                if step >= RING:
                    pool.wait_ge(s_l2, step - RING + 1)
                r = step % RING
                nc.gpsimd.tensor_tensor(z_lo[:, r], z[:, r], z_hi[:, r].bitcast(F32),
                                        ALU.subtract).then_inc(s_z_lo_p, 1)

            pool.wait_ge(s_ids, 16)
            gather(0, range(F))
            gathered(0)
            spots = 5 * KIND.count("pool")
            for t in range(BLOCKS):
                spot = 0
                for k in range(PER_BLOCK):
                    tile = t * PER_BLOCK + k
                    if k == 0 and 1 <= t < BLOCKS - 1:
                        pool.wait_ge(s_staged, t * PER_BLOCK)
                    if k == 5 and t < BLOCKS - 1:
                        gathered(t + 1)
                    for g in range(G):
                        if KIND[g] == "pool":
                            take_rest(tile, g)
                            if spot < spots and t < BLOCKS - 1:
                                gather(t + 1, range(F * spot // spots, F * (spot + 1) // spots))
                                spot += 1

        @block.scalar
        def _(act):
            act.wait_ge(s_w2_in, 16)
            for g in range(0, G, 2):
                nc.scalar.activation(w2_hi[:, g:g + 2].rearrange("p g v n -> p g (v n)"),
                                     w2_raw[:, g:g + 2], ACT.Copy).then_inc(s_w2_hi, 1)

            def x_copies(tile, par):
                act.wait_ge(s_x_t, tile + 1)
                if due(J * (tile - 1)):
                    act.wait_ge(s_z1, J * (tile - 1))
                nc.scalar.activation(x_rep[:, par], x_t[:], ACT.Copy).then_inc(s_x_rep, 1)
                if due(G * (tile - 1)):
                    act.wait_ge(s_spread, G * (tile - 1))
                nc.scalar.activation(x_split[0:F, par], x_t[0:F, :], ACT.Copy).then_inc(s_x_hi, 1)

            def relus(tile, par, some):
                if some[0] == 0:
                    act.wait_ge(s_sum1, tile + 1)
                    act.wait_ge(s_l1, J * (tile + 1))
                    if due(G * (tile - 1)):
                        act.wait_ge(s_z, G * (tile - 1))
                for n in some:
                    v, q = divmod(n, Q)
                    nc.scalar.activation(cur1[F * q:F * (q + 1), par, v], acc1[F * v:F * (v + 1), :],
                                         ACT.Relu).then_inc(s_cur1, 1)

            def round_z(tile, g, step, r):
                act.wait_ge(s_z, step + 1)
                if due(step - RING + 1):
                    act.wait_ge(s_l2, step - RING + 1)
                nc.scalar.activation(z_hi[:, r], z[:, r], ACT.Copy).then_inc(s_z_hi, 1)

            def pair_of_tiles(pair):
                for p in range(2):
                    for g in range(G):
                        tile = 2 * pair + p
                        if g == 2 and live(tile + 2):
                            x_copies(tile + 2, p)
                        if live(tile + 1):
                            if g == 0:
                                relus(tile + 1, 1 - p, range(0, 2))
                            if g == 1:
                                relus(tile + 1, 1 - p, range(2, 7))
                            if g == 2:
                                relus(tile + 1, 1 - p, range(7, 12))
                            if g == 3:
                                relus(tile + 1, 1 - p, range(12, 16))
                        ahead, ga = divmod(g + AHEAD, G)
                        if live(tile + ahead) and KIND[ga] != "plain":
                            round_z(tile + ahead, ga, G * tile + g + AHEAD, (g + AHEAD) % RING)

            over_pairs(act, pair_of_tiles)

            act.wait_ge(s_small_in, 64)
            for m in range(H1 // P):
                act.wait_ge(s_h1, m + 1)
                nc.scalar.activation(hid1[:, m], [x_t, acc1, *rolled][m][:], ACT.Relu,
                                     bias=bias1[:, m:m + 1]).then_inc(s_hid1, 1)
            for m in range(H2 // P):
                act.wait_ge(s_h2, m + 1)
                nc.scalar.activation(hid2[:, m], spread[m][:], ACT.Relu,
                                     bias=bias2[:, m:m + 1]).then_inc(s_hid2, 1)

        @block.vector
        def _(dve):
            nc.vector.memset(sum1[:], 0.0).then_inc(s_zeroed, 1)
            nc.vector.memset(sum2[:], 0.0).then_inc(s_zeroed, 1)
            dve.wait_ge(s_sel_in, 16)
            nc.vector.tensor_copy(sel[:].rearrange("p k n -> p (k n)"), sel_raw).then_inc(s_sel, 1)
            dve.wait_ge(s_w1_in, 32)
            nc.vector.tensor_tensor(w1[:].rearrange("p j n -> p (j n)"),
                                    w1[:].rearrange("p j n -> p (j n)"), w1_back,
                                    ALU.add).then_inc(s_w1, 1)
            for n, g in enumerate(range(0, G, 2)):
                dve.wait_ge(s_w2_hi, n + 1)
                nc.vector.tensor_tensor(
                    w2_lo[:, g:g + 2].rearrange("p g v n -> p g (v n)"), w2_raw[:, g:g + 2],
                    w2_hi[:, g:g + 2].rearrange("p g v n -> p g (v n)").bitcast(F32),
                    ALU.subtract).then_inc(s_w2_lo, 1)
            dve.wait_ge(s_w2_lo, G // 2)
            dve.wait_ge(s_sel, 1)
            dve.wait_ge(s_w1, 1)
            dve.wait_ge(s_zeroed, 2)

            def stage(tile, pair, p):
                block_of, first_d = pair // 4, (pair % 4) * 2 * TD + p * TD
                dve.wait_ge(s_rows, block_of + 1)
                if due(tile - 1):
                    dve.wait_ge(s_x_t, tile - 1)
                nc.vector.tensor_copy(
                    staged[:, p], tile_of_rows(block_of % 2, first_d)).then_inc(s_staged, 1)

            def tile_of_rows(half, first_d):
                src = rows[:, bass.ds(half, 1), :, bass.ds(first_d, TD)]
                return src.rearrange("p o f d -> p d o f").to_broadcast([P, TD, Q, F])

            def x_rest(tile, par):
                dve.wait_ge(s_x_hi, tile + 1)
                dve.wait_ge(s_x_rep, tile + 1)
                nc.vector.tensor_tensor(x_split[F:2 * F, par], x_t[F:2 * F, :],
                                        x_split[0:F, par].bitcast(F32),
                                        ALU.subtract).then_inc(s_x_lo, 1)

            def product1(tile, par, j):
                n = J * tile + j
                dve.wait_ge(s_rolled, n + 1)
                dve.wait_ge(s_x_rep, tile + 1)
                if due(n - 1):
                    dve.wait_ge(s_l1, n - 1)
                k = (J * par + j) % 2
                nc.vector.tensor_tensor(z1[:, k], rolled[k][:], x_rep[:, par],
                                        ALU.mult).then_inc(s_z1, 1)

            def add_relu(total, bank, pair):
                part = total[:, bass.ds(pair // 4, 1), :].rearrange("p o c -> p (o c)")
                return nc.vector.scalar_tensor_tensor(out=part, in0=bank[:], scalar=0.0, in1=part,
                                                      op0=ALU.max, op1=ALU.add)

            def product2(tile, par, g, step, r):
                dve.wait_ge(s_spread, step + 1)
                if g == 0:
                    dve.wait_ge(s_cur1, CUR1 * (tile + 1))
                if due(step - RING + 1):
                    dve.wait_ge(s_l2, step - RING + 1)
                nc.vector.tensor_tensor(
                    z[:, r], spread[g % 2][:].rearrange("p (o c) -> p o c", o=1).to_broadcast(
                        [P, V, COLS]), cur1[:, par], ALU.mult).then_inc(s_z, 1)

            def take_rest(tile, g, step, r):
                dve.wait_ge(s_z_hi, count(("pool", "vector"), tile, g))
                if due(step - RING + 1):
                    dve.wait_ge(s_l2, step - RING + 1)
                nc.vector.tensor_tensor(z_lo[:, r], z[:, r], z_hi[:, r].bitcast(F32),
                                        ALU.subtract).then_inc(s_z_lo_v, 1)

            def pair_of_tiles(pair):
                for p in range(2):
                    tile = 2 * pair + p
                    for g in range(G):
                        ahead, ga = divmod(g + AHEAD, G)
                        if live(tile + ahead):
                            product2(tile + ahead, (p + ahead) % 2, ga, G * tile + g + AHEAD,
                                     (g + AHEAD) % RING)
                        if g == 0 and live(tile + 1):
                            dve.wait_ge(s_l1, J * (tile + 2))
                            if due(tile + 1):
                                dve.wait_ge(s_sum1, tile + 1)
                            add_relu(sum1, acc1, pair + p).then_inc(s_sum1, 1)
                        if g == 0 and live(tile - 1):
                            dve.wait_ge(s_l2, G * tile)
                            if due(tile - 1):
                                dve.wait_ge(s_sum2, tile - 1)
                            add_relu(sum2, acc2[1 - p], pair - 1 + p).then_inc(s_sum2, 1)
                        if g == 1 and live(tile + 2):
                            stage(tile + 2, pair + 1, p)
                        if g == 2 and live(tile + 2):
                            x_rest(tile + 2, p)
                        if g >= 4 and live(tile + 2):
                            for j in [[0, 1], [2], [3], [4]][g - 4]:
                                product1(tile + 2, p, j)
                        ahead, ga = divmod(g + 2, G)
                        if live(tile + ahead) and KIND[ga] == "vector":
                            take_rest(tile + ahead, ga, G * tile + g + 2, (g + 2) % RING)

            over_pairs(dve, pair_of_tiles)

            def over_d(total, layer):
                nc.vector.tensor_reduce(
                    out=sums[:, layer].rearrange("p (t b) -> p t b", t=BLOCKS),
                    in_=total[:].rearrange("p t (d b) -> p t b d", d=TD), op=ALU.add,
                    axis=AXX).then_inc(s_sums, 1)

            dve.wait_ge(s_z, G * (NT - 1))
            dve.wait_ge(s_sum1, NT)
            over_d(sum1, 0)
            dve.wait_ge(s_l2, G * NT)
            dve.wait_ge(s_sum2, NT - 1)
            add_relu(sum2, acc2[(NT - 1) % 2], LAST).then_inc(s_sum2, 1)
            dve.wait_ge(s_sum2, NT)
            over_d(sum2, 1)
            dve.wait_ge(s_y, 1)
            nc.vector.tensor_copy(y_row[:], acc2[0][0:1, :]).then_inc(s_y_row, 1)

        @block.tensor
        def _(pe):
            pe.wait_ge(s_ident, 16)
            pe.wait_ge(s_sel, 1)
            pe.wait_ge(s_w1, 1)
            pe.wait_ge(s_w2_lo, G // 2)
            pe.wait_ge(s_w2_hi, G // 2)
            pe.wait_ge(s_plain_in, 16 * len(plain_steps))

            def transposes(tile, par):
                pe.wait_ge(s_staged, tile + 1)
                if due(tile):
                    pe.wait_ge(s_x_lo, tile)
                    pe.wait_ge(s_x_hi, tile)
                    pe.wait_ge(s_x_rep, tile)
                for d in range(TD):
                    last = nc.tensor.transpose(x_t[:, P * d:P * (d + 1)],
                                               staged[:, par, d].rearrange("p q f -> p (q f)"),
                                               ident[:])
                last.then_inc(s_x_t, 1)

            def roll(tile, par, j):
                if j == 0:
                    pe.wait_ge(s_x_hi, tile + 1)
                    pe.wait_ge(s_x_lo, tile + 1)
                n = J * tile + j
                if due(n - 1):
                    pe.wait_ge(s_z1, n - 1)
                nc.tensor.matmul(rolled[(J * par + j) % 2][:], sel[:, G + j], x_split[:, par],
                                 start=True, stop=True).then_inc(s_rolled, 1)

            def layer1(tile, par, j):
                pe.wait_ge(s_z1, J * tile + j + 1)
                if j == 0 and due(tile):
                    pe.wait_ge(s_cur1, CUR1 * tile)
                    pe.wait_ge(s_sum1, tile)
                nc.tensor.matmul(acc1[:], w1[:, j], z1[:, (J * par + j) % 2],
                                 start=(j == 0), stop=(j == J - 1)).then_inc(s_l1, 1)

            def spread_x(step, par, g):
                if due(step - 1):
                    pe.wait_ge(s_z, step - 1)
                nc.tensor.matmul(spread[g % 2][:], sel[:, g], x_split[:, par],
                                 start=True, stop=True).then_inc(s_spread, 1)

            def layer2_ready(tile, g):
                if g == 0 and due(tile - 1):
                    pe.wait_ge(s_sum2, tile - 1)
                if KIND[g] == "plain":
                    pe.wait_ge(s_z, G * tile + g + 1)
                else:
                    pe.wait_ge(s_z_hi, count(("pool", "vector"), tile, g))
                    if KIND[g] == "pool":
                        pe.wait_ge(s_z_lo_p, count(("pool",), tile, g))
                    else:
                        pe.wait_ge(s_z_lo_v, count(("vector",), tile, g))

            def layer2(par, g, vs):
                bank, r = acc2[par], g % RING
                for v in vs:
                    first, final = g == 0 and v == 0, g == G - 1 and v == V - 1
                    if KIND[g] == "plain":
                        last = nc.tensor.matmul(bank[:], w2_plain[:, plain_steps.index(g), v],
                                                z[:, r, v], start=first, stop=final)
                        continue
                    nc.tensor.matmul(bank[:], w2_hi[:, g, v], z_hi[:, r, v], start=first, stop=False)
                    nc.tensor.matmul(bank[:], w2_lo[:, g, v], z_hi[:, r, v], start=False, stop=False)
                    last = nc.tensor.matmul(bank[:], w2_hi[:, g, v], z_lo[:, r, v], start=False,
                                            stop=final)
                if vs[-1] == V - 1:
                    last.then_inc(s_l2, 1)

            def pair_of_tiles(pair):
                for p in range(2):
                    tile = 2 * pair + p
                    for g in range(G):
                        ahead, ga = divmod(g + AHEAD + 1, G)
                        if live(tile + ahead):
                            spread_x(G * tile + g + AHEAD + 1, (p + ahead) % 2, ga)
                        if g == 2 and live(tile + 2):
                            transposes(tile + 2, p)
                        if g >= 5 and live(tile + 2):
                            layer1(tile + 2, p, g - 5)
                        if g == 0 and live(tile + 1):
                            layer1(tile + 1, 1 - p, 3)
                        if live(tile):
                            layer2_ready(tile, g)
                            layer2(p, g, [0, 1])
                        if g == 0 and live(tile + 1):
                            layer1(tile + 1, 1 - p, 4)
                        if g >= 4 and live(tile + 2):
                            for j in [[0, 1], [2], [3], [4]][g - 4]:
                                roll(tile + 2, p, j)
                        if live(tile):
                            layer2(p, g, [2, 3])

            over_pairs(pe, pair_of_tiles)

            pe.wait_ge(s_small_in, 64)
            pe.wait_ge(s_top1_in, 32)
            pe.wait_ge(s_cur1, CUR1 * NT)
            banks1 = [x_t, acc1, *rolled]
            pe.wait_ge(s_sums, 1)
            for m in range(H1 // P):
                cut = slice(m * P, (m + 1) * P)
                nc.tensor.matmul(banks1[m][:], w_top1[:, 0, cut], sums[:, 0], start=True, stop=False)
                nc.tensor.matmul(banks1[m][:], w_top1[0:DENSE, 2, cut], dense[:], start=False,
                                 stop=False)
            pe.wait_ge(s_sums, 2)
            for m in range(H1 // P):
                nc.tensor.matmul(banks1[m][:], w_top1[:, 1, m * P:(m + 1) * P], sums[:, 1],
                                 start=False, stop=True).then_inc(s_h1, 1)
            pe.wait_ge(s_top2_in, 16)
            for k in range(H1 // P):
                pe.wait_ge(s_hid1, k + 1)
                for m in range(H2 // P):
                    last = nc.tensor.matmul(spread[m][:], w_top2[:, k, m * P:(m + 1) * P],
                                            hid1[:, k], start=(k == 0), stop=(k == H1 // P - 1))
                    if k == H1 // P - 1:
                        last.then_inc(s_h2, 1)
            for k in range(H2 // P):
                pe.wait_ge(s_hid2, k + 1)
                last = nc.tensor.matmul(acc2[0][0:1, :], w_top3[:, k:k + 1], hid2[:, k],
                                        start=(k == 0), stop=(k == H2 // P - 1))
            last.then_inc(s_y, 1)


def selections():
    import numpy as np
    sel = np.zeros((2 * F, G + J, P), np.float32)
    for p in range(P):
        q, i = divmod(p, F)
        for part in range(2):
            for g in range(G):
                sel[part * F + Q * g + q, g, p] = 1
            for j in range(J):
                sel[part * F + (i + Q * j + q) % F, G + j, p] = 1
    return sel.reshape(2 * F, -1)


def layer1_rows():
    import numpy as np
    forth, back = -np.ones((P, J), np.int64), -np.ones((P, J), np.int64)
    for p in range(P):
        q, i = divmod(p, F)
        for j in range(J):
            k = Q * j + q
            if k > F // 2 or (k == F // 2 and i >= F // 2):
                continue
            m = (i + k) % F
            forth[p, j] = i * F + m
            if k:
                back[p, j] = m * F + i
    return forth, back


def kernel(**inputs):
    import numpy as np
    import concourse.bacc as bacc
    from concourse.bass_utils import run_bass_kernel_spmd

    def laid(x):
        return np.ascontiguousarray(x)

    f0 = np.asarray(inputs["L0_rec_filter_0"])[0]
    f1 = np.asarray(inputs["L0_rec_filter_1"])[0]
    with_none = np.concatenate([f0, np.zeros((1, N1), f0.dtype)])
    forth, back = layer1_rows()
    arrays = {
        "ids": laid(np.asarray(inputs["ids"]).reshape(BLOCKS, P, F).transpose(1, 0, 2)),
        "ident": np.eye(P, dtype=np.float32),
        "sel": selections(),
        "w1_forth": laid(with_none[forth].reshape(P, J * N1)),
        "w1_back": laid(with_none[back].reshape(P, J * N1)),
        "w2": laid(f1.reshape(G, Q, V, F, N2).transpose(1, 3, 0, 2, 4).reshape(P, G, V * N2)),
        "dense": laid(np.asarray(inputs["dense_ctx"]).T),
        "b_top1": laid(np.asarray(inputs["b_top1"]).reshape(H1 // P, P).T),
        "b_top2": laid(np.asarray(inputs["b_top2"]).reshape(H2 // P, P).T),
        "w_top1": laid(inputs["W_top1"]),
        "w_top2": laid(inputs["W_top2"]),
        "w_top3": laid(np.asarray(inputs["W_top3"]).reshape(H2 // P, P).T),
    }
    for f in range(F):
        arrays[f"tbl_{f}"] = laid(inputs[f"tbl_{f}"])
    nc = bacc.Bacc("TRN2", target_bir_lowering=False, num_devices=1)
    aps = {k: nc.dram_tensor(f"in_{k}", x.shape, mybir.dt.from_np(x.dtype), kind="ExternalInput").ap()
           for k, x in arrays.items()}
    out = nc.dram_tensor("out_y", (1, B), F32, kind="ExternalOutput").ap()
    tower(nc, aps, [aps[f"tbl_{f}"] for f in range(F)], out)
    r = run_bass_kernel_spmd(nc, [{f"in_{k}": x for k, x in arrays.items()}], core_ids=[0])
    return r.results[0]["out_y"].reshape(B, 1)
```

```python
from contextlib import ExitStack

import concourse.bass as bass
from concourse import mybir

F32 = mybir.dt.float32
F32R = mybir.dt.float32r
I32 = mybir.dt.int32
ALU = mybir.AluOpType
ACT = mybir.ActivationFunctionType
AXX = mybir.AxisListType.X

P = 128
B, F, D = 512, 32, 32
N1 = N2 = 128
DENSE = 16
H1, H2 = 512, 256
Q = P // F
TD = 4
COLS = TD * P
BLOCKS = B // P
PER_BLOCK = D // TD
NT = BLOCKS * PER_BLOCK
G = F // Q
V = N1 // F
W = 2
STEPS = G * V // W
J = 5
RING = 8
AHEAD = 6
REST_AHEAD = 4
SPREAD_AHEAD = 8
K1T = 3

KIND = ["pool", "vector", "pool", "pool", "plain", "pool", "pool", "vector",
        "pool", "pool", "vector", "pool", "plain", "pool", "vector", "pool"]


def count(kinds, tile, s):
    return sum(k in kinds for k in KIND) * tile + sum(k in kinds for k in KIND[:s + 1])


def live(tile):
    return not isinstance(tile, int) or 0 <= tile < NT


def due(n):
    return not isinstance(n, int) or n > 0


def tower(nc, a, tables, out):
    with ExitStack() as ctx:
        def sb(name, shape, dt=F32):
            return ctx.enter_context(nc.sbuf_tensor(name, shape, dt))

        def ps(name, shape=(P, COLS)):
            return ctx.enter_context(nc.psum_tensor(name, list(shape), F32))

        def sem(name):
            return ctx.enter_context(nc.semaphore(name))

        ids = sb("ids_sb", [P, BLOCKS, F], I32)
        rows = sb("rows", [P, 2, F, D])
        ident = sb("ident_sb", [P, P])
        sel = sb("sel_r", [2 * F, G + J, P], F32R)
        w1 = sb("w1", [P, J, N1])
        w2_hi = sb("w2_hi", [P, G, V, N2], F32R)
        w2_lo = sb("w2_lo", [P, G, V, N2], F32R)
        plain_steps = [s for s in range(STEPS) if KIND[s] == "plain"]
        w2_plain = sb("w2_plain", [P, max(1, len(plain_steps)), W, N2])
        dense = sb("dense_sb", [DENSE, B])
        bias1 = sb("bias1", [P, H1 // P])
        bias2 = sb("bias2", [P, H2 // P])
        w_top3 = sb("w_top3_sb", [P, H2 // P])
        staged = sb("staged", [P, 2, TD, Q, F])
        x_split = sb("x_split", [2 * F, 2, COLS], F32R)
        x_rep = sb("x_rep", [P, 2, COLS])
        z1 = sb("z1", [P, 2, COLS])
        cur1 = sb("cur1", [P, 2, V, COLS])
        z = sb("z", [P, RING, W, COLS])
        z_hi = sb("z_hi", [P, RING, W, COLS], F32R)
        z_lo = sb("z_lo", [P, RING, W, COLS], F32R)
        sum1 = sb("sum1", [P, BLOCKS, COLS])
        sum2 = sb("sum2", [P, BLOCKS, COLS])
        y_row = sb("y_row", [1, B])

        w2_raw = z[:, 0:4].rearrange("p r v c -> p (r v c)").rearrange("p (g n) -> p g n", g=G)
        sel_raw = z[0:2 * F, 4:6].rearrange("p r v c -> p (r v c)")[:, 0:(G + J) * P]
        w1_back = z[:, 6].rearrange("p v c -> p (v c)")[:, 0:J * N1]
        w_top1 = rows[:, :].rearrange("p t f d -> p (t f d)")[:, 0:K1T * H1].rearrange(
            "p (k n) -> p k n", k=K1T)
        sums = cur1[:, 0, 0:2]
        w_top2 = cur1[:, 0, 2:4].rearrange("p v c -> p (v c)").rearrange("p (k n) -> p k n", n=H2)
        hid1 = z[:, 0:2].rearrange("p r v c -> p (r v) c")
        hid2 = z[:, 2]

        spread = [ps(f"spread{i}") for i in range(2)]
        rolled = [ps(f"rolled{i}") for i in range(2)]
        x_t = ps("x_t")
        acc1 = ps("acc1")
        acc2 = [ps(f"acc2_{i}") for i in range(2)]

        s_ids = sem("s_ids")
        s_ident = sem("s_ident")
        s_sel_in = sem("s_sel_in")
        s_w1_in = sem("s_w1_in")
        s_w2_in = sem("s_w2_in")
        s_plain_in = sem("s_plain_in")
        s_small_in = sem("s_small_in")
        s_top1_in = sem("s_top1_in")
        s_top2_in = sem("s_top2_in")
        s_gather = [sem(f"s_gather{t}") for t in range(BLOCKS)]
        s_out = sem("s_out")
        s_w2_hi = sem("s_w2_hi")
        s_w2_lo = sem("s_w2_lo")
        s_sel = sem("s_sel")
        s_w1 = sem("s_w1")
        s_zeroed = sem("s_zeroed")
        s_rows = sem("s_rows")
        s_staged = sem("s_staged")
        s_x_t = sem("s_x_t")
        s_x_rep = sem("s_x_rep")
        s_x_hi = sem("s_x_hi")
        s_x_lo = sem("s_x_lo")
        s_rolled = sem("s_rolled")
        s_z1 = sem("s_z1")
        s_l1 = sem("s_l1")
        s_sum1 = sem("s_sum1")
        s_cur1 = sem("s_cur1")
        s_spread = sem("s_spread")
        s_z = sem("s_z")
        s_z_hi = sem("s_z_hi")
        s_z_lo_v = sem("s_z_lo_v")
        s_z_lo_p = sem("s_z_lo_p")
        s_l2 = sem("s_l2")
        s_sum2 = sem("s_sum2")
        s_sums = sem("s_sums")
        s_h1 = sem("s_h1")
        s_hid1 = sem("s_hid1")
        s_h2 = sem("s_h2")
        s_hid2 = sem("s_hid2")
        s_y = sem("s_y")
        s_y_row = sem("s_y_row")

        LAST = NT // 2 - 1
        CUR1 = Q * V

        def over_pairs(eng, pair_of_tiles):
            pair_of_tiles(-1)
            pair_of_tiles(0)
            with eng.Fori(1, LAST) as pair:
                pair_of_tiles(pair)
            pair_of_tiles(LAST)

        block = ctx.enter_context(nc.Block())

        @block.sync
        def _(sp):
            sp.dma_start(ids[:], a["ids"]).then_inc(s_ids, 16)
            sp.dma_start(ident[:], a["ident"]).then_inc(s_ident, 16)
            sp.dma_start(sel_raw, a["sel"]).then_inc(s_sel_in, 16)
            sp.dma_start(w1[:].rearrange("p j n -> p (j n)"), a["w1_forth"]).then_inc(s_w1_in, 16)
            sp.dma_start(w1_back, a["w1_back"]).then_inc(s_w1_in, 16)
            sp.dma_start(w2_raw, a["w2"]).then_inc(s_w2_in, 16)
            for n, s in enumerate(plain_steps):
                g, v = divmod(s * W, V)
                sp.dma_start(w2_plain[:, n].rearrange("p v n -> p (v n)"),
                             a["w2"][:, g, v * N2:(v + W) * N2]).then_inc(s_plain_in, 16)
            sp.dma_start(dense[:], a["dense"]).then_inc(s_small_in, 16)
            sp.dma_start(bias1[:], a["b_top1"]).then_inc(s_small_in, 16)
            sp.dma_start(bias2[:], a["b_top2"]).then_inc(s_small_in, 16)
            sp.dma_start(w_top3[:], a["w_top3"]).then_inc(s_small_in, 16)
            sp.wait_ge(s_staged, NT)
            sp.dma_start(w_top1[:, 0:2], a["w_top1"][0:2 * P].rearrange("(k p) n -> p k n", p=P)
                         ).then_inc(s_top1_in, 16)
            sp.dma_start(w_top1[0:DENSE, 2], a["w_top1"][2 * P:]).then_inc(s_top1_in, 16)
            sp.wait_ge(s_z, STEPS * (NT - 1))
            sp.dma_start(w_top2, a["w_top2"].rearrange("(k p) n -> p k n", p=P)).then_inc(
                s_top2_in, 16)
            sp.wait_ge(s_y_row, 1)
            sp.dma_start(out, y_row[:]).then_inc(s_out, 16)
            sp.wait_ge(s_out, 16)

        @block.gpsimd
        def _(pool):
            def gather(t, fields):
                for f in fields:
                    nc.gpsimd.indirect_dma_start(
                        out=rows[:, t % 2, f, :], out_offset=None, in_=tables[f],
                        in_offset=bass.IndirectOffsetOnAxis(ap=ids[:, t, f:f + 1], axis=0),
                    ).then_inc(s_gather[t], 16)

            def gathered(t):
                pool.wait_ge(s_gather[t], 16 * F)
                pool.sem_inc(s_rows, 1)

            def take_rest(tile, s):
                step = STEPS * tile + s
                pool.wait_ge(s_z_hi, count(("pool", "vector"), tile, s))
                if step >= RING:
                    pool.wait_ge(s_l2, step - RING + 1)
                r = step % RING
                nc.gpsimd.tensor_tensor(z_lo[:, r], z[:, r], z_hi[:, r].bitcast(F32),
                                        ALU.subtract).then_inc(s_z_lo_p, 1)

            pool.wait_ge(s_ids, 16)
            gather(0, range(F))
            gathered(0)
            spots = 5 * KIND.count("pool")
            for t in range(BLOCKS):
                spot = 0
                for k in range(PER_BLOCK):
                    tile = t * PER_BLOCK + k
                    if k == 0 and 1 <= t < BLOCKS - 1:
                        pool.wait_ge(s_staged, t * PER_BLOCK)
                    if k == 5 and t < BLOCKS - 1:
                        gathered(t + 1)
                    for s in range(STEPS):
                        if KIND[s] == "pool":
                            take_rest(tile, s)
                            if spot < spots and t < BLOCKS - 1:
                                gather(t + 1, range(F * spot // spots, F * (spot + 1) // spots))
                                spot += 1

        @block.scalar
        def _(act):
            act.wait_ge(s_w2_in, 16)
            for g in range(0, G, 2):
                nc.scalar.activation(w2_hi[:, g:g + 2].rearrange("p g v n -> p g (v n)"),
                                     w2_raw[:, g:g + 2], ACT.Copy).then_inc(s_w2_hi, 1)

            def x_copies(tile, par):
                act.wait_ge(s_x_t, tile + 1)
                if due(J * (tile - 1)):
                    act.wait_ge(s_z1, J * (tile - 1))
                nc.scalar.activation(x_rep[:, par], x_t[:], ACT.Copy).then_inc(s_x_rep, 1)
                if due(G * (tile - 1)):
                    act.wait_ge(s_spread, G * (tile - 1))
                nc.scalar.activation(x_split[0:F, par], x_t[0:F, :], ACT.Copy).then_inc(s_x_hi, 1)

            def relus(tile, par, some):
                if some[0] == 0:
                    act.wait_ge(s_sum1, tile + 1)
                    act.wait_ge(s_l1, J * (tile + 1))
                    if due(STEPS * (tile - 1)):
                        act.wait_ge(s_z, STEPS * (tile - 1))
                for n in some:
                    v, q = divmod(n, Q)
                    nc.scalar.activation(cur1[F * q:F * (q + 1), par, v], acc1[F * v:F * (v + 1), :],
                                         ACT.Relu).then_inc(s_cur1, 1)

            def round_z(step, r):
                act.wait_ge(s_z, step + 1)
                if due(step - RING + 1):
                    act.wait_ge(s_l2, step - RING + 1)
                nc.scalar.activation(z_hi[:, r], z[:, r], ACT.Copy).then_inc(s_z_hi, 1)

            def pair_of_tiles(pair):
                for p in range(2):
                    tile = 2 * pair + p
                    for s in range(STEPS):
                        if s == 7 and live(tile + 2):
                            x_copies(tile + 2, p)
                        if 2 <= s < 8 and live(tile + 1):
                            relus(tile + 1, 1 - p, [range(0, 3), range(3, 6), range(6, 8),
                                                    range(8, 11), range(11, 14), range(14, 16)][s - 2])
                        ahead, sa = divmod(s + AHEAD, STEPS)
                        if live(tile + ahead) and KIND[sa] != "plain":
                            round_z(STEPS * tile + s + AHEAD, sa % RING)

            over_pairs(act, pair_of_tiles)

            act.wait_ge(s_small_in, 64)
            for m in range(H1 // P):
                act.wait_ge(s_h1, m + 1)
                nc.scalar.activation(hid1[:, m], [x_t, acc1, *rolled][m][:], ACT.Relu,
                                     bias=bias1[:, m:m + 1]).then_inc(s_hid1, 1)
            for m in range(H2 // P):
                act.wait_ge(s_h2, m + 1)
                nc.scalar.activation(hid2[:, m], spread[m][:], ACT.Relu,
                                     bias=bias2[:, m:m + 1]).then_inc(s_hid2, 1)

        @block.vector
        def _(dve):
            nc.vector.memset(sum1[:], 0.0).then_inc(s_zeroed, 1)
            nc.vector.memset(sum2[:], 0.0).then_inc(s_zeroed, 1)
            dve.wait_ge(s_sel_in, 16)
            nc.vector.tensor_copy(sel[:].rearrange("p k n -> p (k n)"), sel_raw).then_inc(s_sel, 1)
            dve.wait_ge(s_w1_in, 32)
            nc.vector.tensor_tensor(w1[:].rearrange("p j n -> p (j n)"),
                                    w1[:].rearrange("p j n -> p (j n)"), w1_back,
                                    ALU.add).then_inc(s_w1, 1)
            for n, g in enumerate(range(0, G, 2)):
                dve.wait_ge(s_w2_hi, n + 1)
                nc.vector.tensor_tensor(
                    w2_lo[:, g:g + 2].rearrange("p g v n -> p g (v n)"), w2_raw[:, g:g + 2],
                    w2_hi[:, g:g + 2].rearrange("p g v n -> p g (v n)").bitcast(F32),
                    ALU.subtract).then_inc(s_w2_lo, 1)
            dve.wait_ge(s_w2_lo, G // 2)
            dve.wait_ge(s_sel, 1)
            dve.wait_ge(s_w1, 1)
            dve.wait_ge(s_zeroed, 2)

            def stage(tile, pair, p):
                block_of, first_d = pair // 4, (pair % 4) * 2 * TD + p * TD
                dve.wait_ge(s_rows, block_of + 1)
                if due(tile - 1):
                    dve.wait_ge(s_x_t, tile - 1)
                nc.vector.tensor_copy(
                    staged[:, p], tile_of_rows(block_of % 2, first_d)).then_inc(s_staged, 1)

            def tile_of_rows(half, first_d):
                src = rows[:, bass.ds(half, 1), :, bass.ds(first_d, TD)]
                return src.rearrange("p o f d -> p d o f").to_broadcast([P, TD, Q, F])

            def x_rest(tile, par):
                dve.wait_ge(s_x_hi, tile + 1)
                dve.wait_ge(s_x_rep, tile + 1)
                nc.vector.tensor_tensor(x_split[F:2 * F, par], x_t[F:2 * F, :],
                                        x_split[0:F, par].bitcast(F32),
                                        ALU.subtract).then_inc(s_x_lo, 1)

            def product1(tile, par, j):
                n = J * tile + j
                dve.wait_ge(s_rolled, n + 1)
                dve.wait_ge(s_x_rep, tile + 1)
                if due(n - 1):
                    dve.wait_ge(s_l1, n - 1)
                k = (J * par + j) % 2
                nc.vector.tensor_tensor(z1[:, k], rolled[k][:], x_rep[:, par],
                                        ALU.mult).then_inc(s_z1, 1)

            def add_relu(total, bank, pair):
                part = total[:, bass.ds(pair // 4, 1), :].rearrange("p o c -> p (o c)")
                return nc.vector.scalar_tensor_tensor(out=part, in0=bank[:], scalar=0.0, in1=part,
                                                      op0=ALU.max, op1=ALU.add)

            def product2(tile, par, s, step):
                dve.wait_ge(s_spread, G * tile + s * W // V + 1)
                if s == 0:
                    dve.wait_ge(s_cur1, CUR1 * (tile + 1))
                if due(step - RING + 1):
                    dve.wait_ge(s_l2, step - RING + 1)
                g, v = divmod(s * W, V)
                nc.vector.tensor_tensor(
                    z[:, s % RING], spread[g % 2][:].rearrange("p (o c) -> p o c", o=1).to_broadcast(
                        [P, W, COLS]), cur1[:, par, v:v + W], ALU.mult).then_inc(s_z, 1)

            def take_rest(tile, s, step):
                dve.wait_ge(s_z_hi, count(("pool", "vector"), tile, s))
                if due(step - RING + 1):
                    dve.wait_ge(s_l2, step - RING + 1)
                r = s % RING
                nc.vector.tensor_tensor(z_lo[:, r], z[:, r], z_hi[:, r].bitcast(F32),
                                        ALU.subtract).then_inc(s_z_lo_v, 1)

            def pair_of_tiles(pair):
                for p in range(2):
                    tile = 2 * pair + p
                    for s in range(STEPS):
                        ahead, sa = divmod(s + AHEAD, STEPS)
                        if live(tile + ahead):
                            product2(tile + ahead, (p + ahead) % 2, sa, STEPS * tile + s + AHEAD)
                        if s == 1 and live(tile + 1):
                            dve.wait_ge(s_l1, J * (tile + 2))
                            if due(tile + 1):
                                dve.wait_ge(s_sum1, tile + 1)
                            add_relu(sum1, acc1, pair + p).then_inc(s_sum1, 1)
                        if s == 2 and live(tile - 1):
                            dve.wait_ge(s_l2, STEPS * tile)
                            if due(tile - 1):
                                dve.wait_ge(s_sum2, tile - 1)
                            add_relu(sum2, acc2[1 - p], pair - 1 + p).then_inc(s_sum2, 1)
                        if s == 0 and live(tile + 2):
                            stage(tile + 2, pair + 1, p)
                        if s == 8 and live(tile + 2):
                            x_rest(tile + 2, p)
                        if 11 <= s < 11 + J and live(tile + 2):
                            product1(tile + 2, p, s - 11)
                        ahead, sa = divmod(s + REST_AHEAD, STEPS)
                        if live(tile + ahead) and KIND[sa] == "vector":
                            take_rest(tile + ahead, sa, STEPS * tile + s + REST_AHEAD)

            over_pairs(dve, pair_of_tiles)

            def over_d(total, layer):
                nc.vector.tensor_reduce(
                    out=sums[:, layer].rearrange("p (t b) -> p t b", t=BLOCKS),
                    in_=total[:].rearrange("p t (d b) -> p t b d", d=TD), op=ALU.add,
                    axis=AXX).then_inc(s_sums, 1)

            dve.wait_ge(s_z, STEPS * (NT - 1))
            dve.wait_ge(s_sum1, NT)
            over_d(sum1, 0)
            dve.wait_ge(s_l2, STEPS * NT)
            dve.wait_ge(s_sum2, NT - 1)
            add_relu(sum2, acc2[(NT - 1) % 2], LAST).then_inc(s_sum2, 1)
            dve.wait_ge(s_sum2, NT)
            over_d(sum2, 1)
            dve.wait_ge(s_y, 1)
            nc.vector.tensor_copy(y_row[:], acc2[0][0:1, :]).then_inc(s_y_row, 1)

        @block.tensor
        def _(pe):
            pe.wait_ge(s_ident, 16)
            pe.wait_ge(s_sel, 1)
            pe.wait_ge(s_w1, 1)
            pe.wait_ge(s_w2_lo, G // 2)
            pe.wait_ge(s_w2_hi, G // 2)
            pe.wait_ge(s_plain_in, 16 * len(plain_steps))

            def transposes(tile, par):
                pe.wait_ge(s_staged, tile + 1)
                if due(tile):
                    pe.wait_ge(s_x_lo, tile)
                    pe.wait_ge(s_x_hi, tile)
                    pe.wait_ge(s_x_rep, tile)
                for d in range(TD):
                    last = nc.tensor.transpose(x_t[:, P * d:P * (d + 1)],
                                               staged[:, par, d].rearrange("p q f -> p (q f)"),
                                               ident[:])
                last.then_inc(s_x_t, 1)

            def roll(tile, par, j):
                if j == 0:
                    pe.wait_ge(s_x_hi, tile + 1)
                    pe.wait_ge(s_x_lo, tile + 1)
                n = J * tile + j
                if due(n - 1):
                    pe.wait_ge(s_z1, n - 1)
                nc.tensor.matmul(rolled[(J * par + j) % 2][:], sel[:, G + j], x_split[:, par],
                                 start=True, stop=True).then_inc(s_rolled, 1)

            def layer1(tile, par, j):
                pe.wait_ge(s_z1, J * tile + j + 1)
                if j == 0 and due(tile):
                    pe.wait_ge(s_cur1, CUR1 * tile)
                    pe.wait_ge(s_sum1, tile)
                nc.tensor.matmul(acc1[:], w1[:, j], z1[:, (J * par + j) % 2],
                                 start=(j == 0), stop=(j == J - 1)).then_inc(s_l1, 1)

            def spread_x(tile, par, g):
                readers = STEPS * tile + (g - 1) * (V // W)
                if due(readers):
                    pe.wait_ge(s_z, readers)
                nc.tensor.matmul(spread[g % 2][:], sel[:, g], x_split[:, par],
                                 start=True, stop=True).then_inc(s_spread, 1)

            def layer2_ready(tile, s):
                if s == 0 and due(tile - 1):
                    pe.wait_ge(s_sum2, tile - 1)
                if KIND[s] == "plain":
                    pe.wait_ge(s_z, STEPS * tile + s + 1)
                else:
                    pe.wait_ge(s_z_hi, count(("pool", "vector"), tile, s))
                    if KIND[s] == "pool":
                        pe.wait_ge(s_z_lo_p, count(("pool",), tile, s))
                    else:
                        pe.wait_ge(s_z_lo_v, count(("vector",), tile, s))

            def layer2(par, s):
                bank, r = acc2[par], s % RING
                for w in range(W):
                    g, v = divmod(s * W + w, V)
                    first, final = s == 0 and w == 0, s == STEPS - 1 and w == W - 1
                    if KIND[s] == "plain":
                        last = nc.tensor.matmul(bank[:], w2_plain[:, plain_steps.index(s), w],
                                                z[:, r, w], start=first, stop=final)
                        continue
                    nc.tensor.matmul(bank[:], w2_hi[:, g, v], z_hi[:, r, w], start=first, stop=False)
                    nc.tensor.matmul(bank[:], w2_lo[:, g, v], z_hi[:, r, w], start=False, stop=False)
                    last = nc.tensor.matmul(bank[:], w2_hi[:, g, v], z_lo[:, r, w], start=False,
                                            stop=final)
                last.then_inc(s_l2, 1)

            def pair_of_tiles(pair):
                for p in range(2):
                    tile = 2 * pair + p
                    for s in range(STEPS):
                        ahead, sa = divmod(s + SPREAD_AHEAD, STEPS)
                        if sa * W % V == 0 and live(tile + ahead):
                            spread_x(tile + ahead, (p + ahead) % 2, sa * W // V)
                        if s == 3 and live(tile + 2):
                            transposes(tile + 2, p)
                        if s >= 12 and live(tile + 2):
                            layer1(tile + 2, p, s - 12)
                        if s == 0 and live(tile + 1):
                            layer1(tile + 1, 1 - p, J - 1)
                        if 10 <= s < 10 + J and live(tile + 2):
                            roll(tile + 2, p, s - 10)
                        if live(tile):
                            layer2_ready(tile, s)
                            layer2(p, s)

            over_pairs(pe, pair_of_tiles)

            pe.wait_ge(s_small_in, 64)
            pe.wait_ge(s_top1_in, 32)
            pe.wait_ge(s_cur1, CUR1 * NT)
            banks1 = [x_t, acc1, *rolled]
            pe.wait_ge(s_sums, 1)
            for m in range(H1 // P):
                cut = slice(m * P, (m + 1) * P)
                nc.tensor.matmul(banks1[m][:], w_top1[:, 0, cut], sums[:, 0], start=True, stop=False)
                nc.tensor.matmul(banks1[m][:], w_top1[0:DENSE, 2, cut], dense[:], start=False,
                                 stop=False)
            pe.wait_ge(s_sums, 2)
            for m in range(H1 // P):
                nc.tensor.matmul(banks1[m][:], w_top1[:, 1, m * P:(m + 1) * P], sums[:, 1],
                                 start=False, stop=True).then_inc(s_h1, 1)
            pe.wait_ge(s_top2_in, 16)
            for k in range(H1 // P):
                pe.wait_ge(s_hid1, k + 1)
                for m in range(H2 // P):
                    last = nc.tensor.matmul(spread[m][:], w_top2[:, k, m * P:(m + 1) * P],
                                            hid1[:, k], start=(k == 0), stop=(k == H1 // P - 1))
                    if k == H1 // P - 1:
                        last.then_inc(s_h2, 1)
            for k in range(H2 // P):
                pe.wait_ge(s_hid2, k + 1)
                last = nc.tensor.matmul(acc2[0][0:1, :], w_top3[:, k:k + 1], hid2[:, k],
                                        start=(k == 0), stop=(k == H2 // P - 1))
            last.then_inc(s_y, 1)


def selections():
    import numpy as np
    sel = np.zeros((2 * F, G + J, P), np.float32)
    for p in range(P):
        q, i = divmod(p, F)
        for part in range(2):
            for g in range(G):
                sel[part * F + Q * g + q, g, p] = 1
            for j in range(J):
                sel[part * F + (i + Q * j + q) % F, G + j, p] = 1
    return sel.reshape(2 * F, -1)


def layer1_rows():
    import numpy as np
    forth, back = -np.ones((P, J), np.int64), -np.ones((P, J), np.int64)
    for p in range(P):
        q, i = divmod(p, F)
        for j in range(J):
            k = Q * j + q
            if k > F // 2 or (k == F // 2 and i >= F // 2):
                continue
            m = (i + k) % F
            forth[p, j] = i * F + m
            if k:
                back[p, j] = m * F + i
    return forth, back


def kernel(**inputs):
    import numpy as np
    import concourse.bacc as bacc
    from concourse.bass_utils import run_bass_kernel_spmd

    def laid(x):
        return np.ascontiguousarray(x)

    f0 = np.asarray(inputs["L0_rec_filter_0"])[0]
    f1 = np.asarray(inputs["L0_rec_filter_1"])[0]
    with_none = np.concatenate([f0, np.zeros((1, N1), f0.dtype)])
    forth, back = layer1_rows()
    arrays = {
        "ids": laid(np.asarray(inputs["ids"]).reshape(BLOCKS, P, F).transpose(1, 0, 2)),
        "ident": np.eye(P, dtype=np.float32),
        "sel": selections(),
        "w1_forth": laid(with_none[forth].reshape(P, J * N1)),
        "w1_back": laid(with_none[back].reshape(P, J * N1)),
        "w2": laid(f1.reshape(G, Q, V, F, N2).transpose(1, 3, 0, 2, 4).reshape(P, G, V * N2)),
        "dense": laid(np.asarray(inputs["dense_ctx"]).T),
        "b_top1": laid(np.asarray(inputs["b_top1"]).reshape(H1 // P, P).T),
        "b_top2": laid(np.asarray(inputs["b_top2"]).reshape(H2 // P, P).T),
        "w_top1": laid(inputs["W_top1"]),
        "w_top2": laid(inputs["W_top2"]),
        "w_top3": laid(np.asarray(inputs["W_top3"]).reshape(H2 // P, P).T),
    }
    for f in range(F):
        arrays[f"tbl_{f}"] = laid(inputs[f"tbl_{f}"])
    nc = bacc.Bacc("TRN2", target_bir_lowering=False, num_devices=1)
    aps = {k: nc.dram_tensor(f"in_{k}", x.shape, mybir.dt.from_np(x.dtype), kind="ExternalInput").ap()
           for k, x in arrays.items()}
    out = nc.dram_tensor("out_y", (1, B), F32, kind="ExternalOutput").ap()
    tower(nc, aps, [aps[f"tbl_{f}"] for f in range(F)], out)
    r = run_bass_kernel_spmd(nc, [{f"in_{k}": x for k, x in arrays.items()}], core_ids=[0])
    return r.results[0]["out_y"].reshape(B, 1)
```

```python
from contextlib import ExitStack

import concourse.bass as bass
from concourse import mybir

F32 = mybir.dt.float32
F32R = mybir.dt.float32r
I32 = mybir.dt.int32
ALU = mybir.AluOpType
ACT = mybir.ActivationFunctionType
AXX = mybir.AxisListType.X

P = 128
B, F, D = 512, 32, 32
N1 = N2 = 128
DENSE = 16
H1, H2 = 512, 256
Q = P // F
TD = 4
COLS = TD * P
BLOCKS = B // P
PER_BLOCK = D // TD
PAIRS = PER_BLOCK // 2
NT = BLOCKS * PER_BLOCK
HG = COLS // N2
G = F // HG
WAYS = 2
ED = TD // WAYS
STEPS = G * WAYS
PER_STEP = HG * ED
UNITS = G * PER_STEP
J = 5
REST = ["vector", "vector", "vector", "vector", "vector"]
EARLY = 26
GATHER_TILES = 8
K1T = 3

STAGE = 5
X_T = 8
X_REP = 9
PRODUCT = [14, 16, 18, 22, 22]
Z1_HI = [15, 17, 19, 23, 23]
Z1_LO = [16, 18, 20, 24, 24]
LAYER1 = [18, 20, 22, 26, 27]
CUR1_HI = 27
CUR1_LO = 28
SUM1 = 30
SCALE = 29
SUM2_V = 12
SUM2_P = 10

USES = [(p, s, use) for p in range(2) for s in range(STEPS)
        for use in (["x_t"] if s == X_T else []) + list(range(ED))]
ROUNDS = [7, 7, 6, 6, 7, 7, 7, 6, 6, 7]
BANK_OF = [bank for banks in ROUNDS for bank in range(banks)]

TERMS = 4
TERMS_AT = [n % TERMS for n in range(2 * (G - 1))]


def since(places, n):
    return next(k for k in range(1, len(places) + 1) if places[n - k] == places[n])


def rests(engine, tile, j):
    return REST.count(engine) * tile + REST[:j + 1].count(engine)


def live(tile):
    return not isinstance(tile, int) or 0 <= tile < NT


def due(n):
    return not isinstance(n, int) or n > 0


def tower(nc, a, tables, out):
    with ExitStack() as ctx:
        def sb(name, shape, dt=F32):
            return ctx.enter_context(nc.sbuf_tensor(name, shape, dt))

        def ps(name, shape=(P, COLS)):
            return ctx.enter_context(nc.psum_tensor(name, list(shape), F32))

        def sem(name):
            return ctx.enter_context(nc.semaphore(name))

        ids = sb("ids_sb", [P, BLOCKS, F], I32)
        next_ids = sb("next_ids", [P, F], I32)
        next_rows = sb("next_rows", [P, F, D])
        rows = sb("rows", [P, BLOCKS, F, D])
        ident = sb("ident_sb", [P, P])
        w1 = sb("w1", [P, J, N1])
        w1_back = sb("w1_back", [P, J, N1])
        w1_hi = sb("w1_hi", [P, J, N1], F32R)
        w1_lo = sb("w1_lo", [P, J - 1, N1], F32R)
        w2 = sb("w2", [P, G, COLS])
        w2_hi = sb("w2_hi", [P, G, COLS], F32R)
        w2_lo = sb("w2_lo", [P, G, COLS], F32R)
        dense = sb("dense_sb", [DENSE, B])
        bias1 = sb("bias1", [P, H1 // P])
        bias2 = sb("bias2", [P, H2 // P])
        w_top1 = sb("w_top1_sb", [P, K1T, H1])
        w_top2 = sb("w_top2_sb", [P, H1 // P, H2])
        w_top3 = sb("w_top3_sb", [P, H2 // P])
        staged = sb("staged", [P, TD, Q, F])
        x_rep = sb("x_rep", [P, COLS])
        rolled = sb("rolled", [P, J, COLS])
        z1 = sb("z1", [P, J, COLS])
        z1_hi = sb("z1_hi", [P, J, COLS], F32R)
        z1_lo = sb("z1_lo", [P, J, COLS], F32R)
        cur1_hi = sb("cur1_hi", [P, 2, COLS], F32R)
        cur1_lo = sb("cur1_lo", [P, 2, COLS], F32R)
        sum1 = sb("sum1", [P, BLOCKS, COLS])
        scale = sb("scale", [P, 2, F, TD])
        acc2_v = sb("acc2_v", [P, 2, ED, N2])
        terms = sb("terms", [P, TERMS, ED, HG, N2])
        acc4_p = sb("acc4_p", [P, 2, ED, HG, N2])
        acc2_p = sb("acc2_p", [P, 2, ED, N2])
        sum2_v = sb("sum2_v", [P, BLOCKS, ED, N2])
        sum2_p = sb("sum2_p", [P, BLOCKS, ED, N2])
        sums = sb("sums", [P, 2, B])
        hid1 = sb("hid1", [P, H1 // P, B])
        hid2 = sb("hid2", [P, H2 // P, B])
        y_row = sb("y_row", [1, B])

        banks = [ps(f"bank{i}") for i in range(max(ROUNDS))]
        acc1 = ps("acc1")
        by_age = [banks[k] for k in BANK_OF[-max(ROUNDS):]]
        banks_h1, banks_h2, bank_y = by_age[0:4], by_age[4:6], by_age[6]

        def bank_of(p, s, use):
            return banks[BANK_OF[USES.index((p, s, use))]]

        s_ids = sem("s_ids")
        s_ident = sem("s_ident")
        s_w1_in = sem("s_w1_in")
        s_w2_in = sem("s_w2_in")
        s_top_in = sem("s_top_in")
        s_gather = sem("s_gather")
        s_out = sem("s_out")
        s_w2_hi = sem("s_w2_hi")
        s_w2_lo = sem("s_w2_lo")
        s_w1 = sem("s_w1")
        s_w1_hi = sem("s_w1_hi")
        s_w1_lo = sem("s_w1_lo")
        s_zeroed = sem("s_zeroed")
        s_next_ids = sem("s_next_ids")
        s_rows = sem("s_rows")
        s_staged = sem("s_staged")
        s_x_t = sem("s_x_t")
        s_x_rep = sem("s_x_rep")
        s_rolled = [sem(f"s_rolled{j}") for j in range(J)]
        s_scale = sem("s_scale")
        s_z1 = sem("s_z1")
        s_z1_hi = sem("s_z1_hi")
        s_z1_lo_v = sem("s_z1_lo_v")
        s_z1_lo_p = sem("s_z1_lo_p")
        s_l1 = sem("s_l1")
        s_cur1_hi = sem("s_cur1_hi")
        s_cur1_lo = sem("s_cur1_lo")
        s_sum1 = sem("s_sum1")
        s_mixed = sem("s_mixed")
        s_added_v = sem("s_added_v")
        s_terms = sem("s_terms")
        s_added_p = sem("s_added_p")
        s_last_terms = sem("s_last_terms")
        s_folded = sem("s_folded")
        s_sum2_v = sem("s_sum2_v")
        s_sum2_p = sem("s_sum2_p")
        s_sums1 = sem("s_sums1")
        s_turned = sem("s_turned")
        s_sums2 = sem("s_sums2")
        s_h1 = sem("s_h1")
        s_hid1 = sem("s_hid1")
        s_h2 = sem("s_h2")
        s_hid2 = sem("s_hid2")
        s_y = sem("s_y")
        s_y_row = sem("s_y_row")

        LAST = NT // 2 - 1

        def over_pairs(eng, pair_of_tiles):
            pair_of_tiles(-1)
            pair_of_tiles(0)
            with eng.Fori(1, LAST) as pair:
                pair_of_tiles(pair)
            pair_of_tiles(LAST)

        def layer1_work(pair, p, s, at):
            first = at < STEPS
            if at % STEPS != s or not live(2 * pair + p + (2 if first else 1)):
                return []
            if first:
                return [(2 * pair + p + 2, pair + 1, p)]
            return [(2 * pair + p + 1, pair + p, 1 - p)]

        def coordinates(pair, p):
            return (pair % PAIRS) * 2 * TD + p * TD

        def rows_of(pair, p):
            return rows[:, bass.ds(pair // PAIRS, 1), :, bass.ds(coordinates(pair, p), TD)]

        def z1_lo_ready(eng, tile, j):
            engine = REST[j]
            eng.wait_ge({"vector": s_z1_lo_v, "pool": s_z1_lo_p}[engine], rests(engine, tile, j))

        def take_rest1(eng, tile, j):
            eng.wait_ge(s_z1_hi, J * tile + j + 1)
            dest, some = (z1_lo, slice(0, P)) if j < J - 1 else (z1_hi, slice(F, 2 * F))
            return eng.tensor_tensor(dest[some, j], z1[some, j], z1_hi[some, j].bitcast(F32),
                                     ALU.subtract)

        def add_relu(eng, total, src, pair):
            part = total[:, bass.ds(pair // PAIRS, 1)]
            if len(part.shape) == 4:
                part = part.rearrange("p o d n -> p (o d) n")
            else:
                part = part.rearrange("p o c -> p (o c)")
            return eng.scalar_tensor_tensor(out=part, in0=src, scalar=0.0, in1=part,
                                            op0=ALU.max, op1=ALU.add)

        block = ctx.enter_context(nc.Block())

        @block.sync
        def _(sp):
            sp.dma_start(ids[:], a["ids"]).then_inc(s_ids, 16)
            sp.dma_start(ident[:], a["ident"]).then_inc(s_ident, 16)
            sp.dma_start(w1[:].rearrange("p j n -> p (j n)"), a["w1_forth"]).then_inc(s_w1_in, 16)
            sp.dma_start(w1_back[:].rearrange("p j n -> p (j n)"), a["w1_back"]).then_inc(
                s_w1_in, 16)
            sp.dma_start(w2[:], a["w2"]).then_inc(s_w2_in, 16)
            sp.dma_start(dense[:], a["dense"]).then_inc(s_top_in, 16)
            sp.dma_start(bias1[:], a["b_top1"]).then_inc(s_top_in, 16)
            sp.dma_start(bias2[:], a["b_top2"]).then_inc(s_top_in, 16)
            sp.dma_start(w_top3[:], a["w_top3"]).then_inc(s_top_in, 16)
            sp.dma_start(w_top1[:, 0:2], a["w_top1"][0:2 * P].rearrange("(k p) n -> p k n", p=P)
                         ).then_inc(s_top_in, 16)
            sp.dma_start(w_top1[0:DENSE, 2], a["w_top1"][2 * P:]).then_inc(s_top_in, 16)
            sp.dma_start(w_top2[:], a["w_top2"].rearrange("(k p) n -> p k n", p=P)).then_inc(
                s_top_in, 16)

            def shift(tile):
                sp.wait_ge(s_x_rep, tile + 1)
                for j in range(J - 1):
                    if due(tile):
                        sp.wait_ge(s_z1, J * (tile - 1) + j + 1)
                    for q in range(Q):
                        k = Q * j + q
                        sp.dma_start(rolled[F * q:F * (q + 1), j], x_rep[k:k + F]).then_inc(
                            s_rolled[j], 16)
                if due(tile):
                    sp.wait_ge(s_z1, J * tile)
                sp.dma_start(rolled[0:3 * F, J - 1], x_rep[F // 2:F // 2 + 3 * F]).then_inc(
                    s_rolled[J - 1], 16)

            shift(0)
            with sp.Fori(1, NT) as tile:
                shift(tile)
            sp.wait_ge(s_y_row, 1)
            sp.dma_start(out, y_row[:]).then_inc(s_out, 16)
            sp.wait_ge(s_out, 16)

        TOP_IN = 7 * 16

        @block.gpsimd
        def _(pool):
            def gather(dest, of_ids, fields):
                for f in fields:
                    nc.gpsimd.indirect_dma_start(
                        out=dest[:, f, :], out_offset=None, in_=tables[f],
                        in_offset=bass.IndirectOffsetOnAxis(ap=of_ids[:, f:f + 1], axis=0),
                    ).then_inc(s_gather, 16)

            def spots(fields, n):
                return [fields[len(fields) * k // n:len(fields) * (k + 1) // n] for k in range(n)]

            def take_ids(t):
                nc.gpsimd.tensor_copy(
                    next_ids[:], ids[:, bass.ds(t, 1)].rearrange("p o f -> p (o f)")
                ).then_inc(s_next_ids, 1)
                pool.wait_ge(s_next_ids, t - 1)
                pool.wait_ge(s_rows, t)

            def move_rows(t):
                pool.wait_ge(s_gather, 16 * F * (t + 1))
                nc.gpsimd.tensor_copy(rows[:, bass.ds(t, 1)].rearrange("p o f d -> p (o f) d"),
                                      next_rows[:]).then_inc(s_rows, 1)

            def add_terms(tile, par, g):
                pool.wait_ge(s_terms, ED * (G * tile + g + 1))
                if g > 1:
                    pool.wait_ge(s_added_p, (G - 1) * tile + g - 1)
                place = TERMS_AT[(G - 1) * par + g - 1]
                nc.gpsimd.tensor_tensor(acc4_p[:, par], acc4_p[:, par], terms[:, place],
                                        ALU.add).then_inc(s_added_p, 1)

            def fold(tile, par):
                pool.wait_ge(s_added_p, (G - 1) * (tile + 1))
                nc.gpsimd.tensor_tensor(acc4_p[:, par, :, 0:2], acc4_p[:, par, :, 0:2],
                                        acc4_p[:, par, :, 2:4], ALU.add).then_inc(s_folded, 1)
                pool.wait_ge(s_folded, 2 * tile + 1)
                if due(tile - 1):
                    pool.wait_ge(s_sum2_p, tile - 1)
                nc.gpsimd.tensor_tensor(acc2_p[:, par], acc4_p[:, par, :, 0],
                                        acc4_p[:, par, :, 1], ALU.add).then_inc(s_folded, 1)

            def tile_work(pair, p, gathers=(), t=None):
                tile = 2 * pair + p
                for s in range(STEPS):
                    for j in range(J):
                        for u, _, _ in layer1_work(pair, p, s, Z1_LO[j]):
                            if REST[j] == "pool":
                                take_rest1(nc.gpsimd, u, j).then_inc(s_z1_lo_p, 1)
                    is_last = isinstance(tile, int) and tile == NT - 1 and s == STEPS - 1
                    if live(tile) and s % WAYS == 1 and s > 1 and not is_last:
                        add_terms(tile, p, s // WAYS)
                    if s == 1 and live(tile - 1):
                        fold(tile - 1, 1 - p)
                    if s % WAYS == 1 and gathers:
                        if t is None:
                            gather(next_rows, next_ids, gathers[s // WAYS])
                        else:
                            gather(rows[:, t], ids[:, t], gathers[s // WAYS])

            pool.wait_ge(s_ids, 16)
            gather(rows[:, 0], ids[:, 0], range(F))
            pool.wait_ge(s_gather, 16 * F)
            pool.sem_inc(s_rows, 1)
            gather(rows[:, 1], ids[:, 1], range(EARLY))
            tile_work(-1, 0)
            tile_work(-1, 1)
            tile_work(0, 0, spots(range(EARLY, F), G), 1)
            pool.wait_ge(s_gather, 16 * F * 2)
            pool.sem_inc(s_rows, 1)
            tile_work(0, 1)
            with pool.Fori(1, PAIRS - 1) as pair:
                tile_work(pair, 0)
                tile_work(pair, 1)

            with pool.Fori(1, BLOCKS - 1) as t:
                take_ids(t + 1)
                some = spots(range(F), GATHER_TILES * G)
                for k in range(PER_BLOCK):
                    tile_work(t * PAIRS - 1 + k // 2, k % 2, some[k * G:(k + 1) * G])
                move_rows(t + 1)
            first = (BLOCKS - 1) * PAIRS - 1
            with pool.Fori(first, LAST) as pair:
                tile_work(pair, 0)
                tile_work(pair, 1)
            tile_work(LAST, 0)
            tile_work(LAST, 1)

        @block.scalar
        def _(act):
            act.wait_ge(s_w2_in, 16)
            for g in range(0, G, 2):
                nc.scalar.activation(w2_hi[:, g:g + 2], w2[:, g:g + 2], ACT.Copy).then_inc(
                    s_w2_hi, 1)
            act.wait_ge(s_w1, 1)
            nc.scalar.activation(w1_hi[:], w1[:], ACT.Copy).then_inc(s_w1_hi, 1)

            def stage(tile, pair, p):
                act.wait_ge(s_rows, pair // PAIRS + 1)
                if due(tile):
                    act.wait_ge(s_x_t, tile)
                src = rows_of(pair, p).rearrange("p o f d -> p d o f")
                nc.scalar.activation(staged[:], src.to_broadcast([P, TD, Q, F]),
                                     ACT.Copy).then_inc(s_staged, 1)

            def copy_scale(tile, pair, p):
                nc.scalar.activation(scale[:, p],
                                     rows_of(pair, p).rearrange("p o f d -> p (o f) d"),
                                     ACT.Copy).then_inc(s_scale, 1)

            def copy_x(tile, par):
                act.wait_ge(s_x_t, tile + 1)
                if due(tile):
                    act.wait_ge(s_z1, J * tile)
                nc.scalar.activation(x_rep[:], bank_of(par, X_T, "x_t")[:],
                                     ACT.Copy).then_inc(s_x_rep, 1)

            def round_z1(tile, j):
                act.wait_ge(s_z1, J * tile + j + 1)
                nc.scalar.activation(z1_hi[:, j], z1[:, j], ACT.Copy).then_inc(s_z1_hi, 1)

            def relu_hi(tile, par):
                act.wait_ge(s_l1, J * (tile + 1))
                if due(tile - 1):
                    act.wait_ge(s_mixed, ED * STEPS * (tile - 1))
                nc.scalar.activation(cur1_hi[:, par], acc1[:], ACT.Relu).then_inc(s_cur1_hi, 1)

            def make_terms(tile, par, s):
                g = s // WAYS
                act.wait_ge(s_scale, tile + 1)
                if g == 0 and due(tile - 1):
                    act.wait_ge(s_folded, 2 * (tile - 1))
                if g > 0:
                    place = (G - 1) * par + g - 1
                    readers = (G - 1) * tile + g - since(TERMS_AT, place)
                    if due(readers):
                        act.wait_ge(s_added_p, readers)
                dest = acc4_p[:, par] if g == 0 else terms[:, TERMS_AT[place]]
                for c in range(ED):
                    act.wait_ge(s_mixed, ED * (STEPS * tile + s) + c + 1)
                    bank = bank_of(par, s, c)
                    for hh in range(HG):
                        h, d = HG * g + hh, ED * (s % WAYS) + c
                        last = nc.scalar.activation(dest[:, c, hh], bank[:, N2 * hh:N2 * (hh + 1)],
                                                    ACT.Copy, scale=scale[:, par, h, d:d + 1])
                    last.then_inc(s_terms, 1)

            def pair_of_tiles(pair):
                for p in range(2):
                    for s in range(STEPS):
                        for tile, its_pair, par in layer1_work(pair, p, s, STAGE):
                            stage(tile, its_pair, par)
                        for tile, its_pair, par in layer1_work(pair, p, s, SCALE):
                            copy_scale(tile, its_pair, par)
                        for tile, _, par in layer1_work(pair, p, s, X_REP):
                            copy_x(tile, par)
                        for j in range(J):
                            for tile, _, _ in layer1_work(pair, p, s, Z1_HI[j]):
                                round_z1(tile, j)
                        for tile, _, par in layer1_work(pair, p, s, CUR1_HI):
                            relu_hi(tile, par)
                        if live(2 * pair + p) and s % WAYS == 1:
                            make_terms(2 * pair + p, p, s)

            over_pairs(act, pair_of_tiles)

            act.wait_ge(s_turned, 1)
            nc.scalar.activation(sums[:, 1], acc1[:], ACT.Copy).then_inc(s_sums2, 1)
            act.wait_ge(s_top_in, TOP_IN)
            for m in range(H1 // P):
                act.wait_ge(s_h1, m + 1)
                nc.scalar.activation(hid1[:, m], banks_h1[m][:], ACT.Relu,
                                     bias=bias1[:, m:m + 1]).then_inc(s_hid1, 1)
            for m in range(H2 // P):
                act.wait_ge(s_h2, m + 1)
                nc.scalar.activation(hid2[:, m], banks_h2[m][:], ACT.Relu,
                                     bias=bias2[:, m:m + 1]).then_inc(s_hid2, 1)

        @block.vector
        def _(dve):
            for total in (sum1, sum2_v, sum2_p):
                nc.vector.memset(total[:], 0.0).then_inc(s_zeroed, 1)
            nc.vector.memset(rolled[3 * F:, J - 1], 0.0).then_inc(s_zeroed, 1)
            dve.wait_ge(s_w1_in, 32)
            nc.vector.tensor_tensor(w1[:], w1[:], w1_back[:], ALU.add).then_inc(s_w1, 1)
            for n, g in enumerate(range(0, G, 2)):
                dve.wait_ge(s_w2_hi, n + 1)
                nc.vector.tensor_tensor(w2_lo[:, g:g + 2], w2[:, g:g + 2],
                                        w2_hi[:, g:g + 2].bitcast(F32), ALU.subtract).then_inc(
                                            s_w2_lo, 1)
            dve.wait_ge(s_w1_hi, 1)
            nc.vector.tensor_tensor(w1_lo[:], w1[:, 0:J - 1], w1_hi[:, 0:J - 1].bitcast(F32),
                                    ALU.subtract).then_inc(s_w1_lo, 1)
            nc.vector.tensor_tensor(w1_hi[2 * F:3 * F, J - 1], w1[2 * F:3 * F, J - 1],
                                    w1_hi[2 * F:3 * F, J - 1].bitcast(F32),
                                    ALU.subtract).then_inc(s_w1_lo, 1)
            dve.wait_ge(s_zeroed, 4)

            def product1(tile, j):
                dve.wait_ge(s_rolled[j], 16 * (Q if j < J - 1 else 1) * (tile + 1))
                if due(tile):
                    dve.wait_ge(s_l1, J * (tile - 1) + j + 1)
                nc.vector.tensor_tensor(z1[:, j], rolled[:, j], x_rep[:], ALU.mult).then_inc(
                    s_z1, 1)

            def relu_lo(tile, par):
                dve.wait_ge(s_cur1_hi, tile + 1)
                nc.vector.scalar_tensor_tensor(
                    out=cur1_lo[:, par], in0=acc1[:], scalar=0.0, in1=cur1_hi[:, par].bitcast(F32),
                    op0=ALU.max, op1=ALU.subtract).then_inc(s_cur1_lo, 1)

            def sum_relu1(tile, pair):
                if due(tile):
                    dve.wait_ge(s_sum1, tile)
                dve.wait_ge(s_cur1_hi, tile + 1)
                add_relu(nc.vector, sum1, acc1[:], pair).then_inc(s_sum1, 1)

            def add_step(tile, par, s):
                g, way = divmod(s, WAYS)
                dve.wait_ge(s_mixed, ED * (STEPS * tile + s + 1))
                if g == 0:
                    dve.wait_ge(s_scale, tile + 1)
                    if due(tile - 1):
                        dve.wait_ge(s_sum2_v, tile - 1)
                for hh in range(HG):
                    for c in range(ED):
                        h, d = HG * g + hh, ED * way + c
                        src = bank_of(par, s, c)[:, N2 * hh:N2 * (hh + 1)]
                        total = acc2_v[:, par, c]
                        x_h = scale[:, par, h, d:d + 1]
                        if h == 0:
                            nc.vector.tensor_scalar(total, src, x_h, None, ALU.mult).then_inc(
                                s_added_v, 1)
                            continue
                        dve.wait_ge(s_added_v, UNITS * tile + ED * h + c - ED + 1)
                        nc.vector.scalar_tensor_tensor(
                            out=total, in0=src, scalar=x_h, in1=total, op0=ALU.mult,
                            op1=ALU.add).then_inc(s_added_v, 1)

            def sum_relu2_v(tile, pair, par):
                dve.wait_ge(s_added_v, UNITS * (tile + 1))
                if due(tile):
                    dve.wait_ge(s_sum2_v, tile)
                add_relu(nc.vector, sum2_v, acc2_v[:, par], pair).then_inc(s_sum2_v, 1)

            def last_terms(par):
                four = acc4_p[:, par]
                dve.wait_ge(s_terms, ED * G * NT)
                dve.wait_ge(s_added_p, (G - 1) * NT - 1)
                nc.vector.tensor_tensor(four, four, terms[:, TERMS_AT[(G - 1) * par + G - 2]],
                                        ALU.add).then_inc(s_last_terms, 1)
                dve.wait_ge(s_last_terms, 1)
                nc.vector.tensor_tensor(four[:, :, 0:2], four[:, :, 0:2], four[:, :, 2:4],
                                        ALU.add).then_inc(s_last_terms, 1)
                dve.wait_ge(s_last_terms, 2)
                nc.vector.tensor_tensor(acc2_p[:, par], four[:, :, 0], four[:, :, 1],
                                        ALU.add).then_inc(s_last_terms, 1)
                dve.wait_ge(s_last_terms, 3)

            def sum_relu2_p(tile, pair, par):
                if not isinstance(tile, int) or tile < NT - 1:
                    dve.wait_ge(s_folded, 2 * (tile + 1))
                if due(tile):
                    dve.wait_ge(s_sum2_p, tile)
                add_relu(nc.vector, sum2_p, acc2_p[:, par], pair).then_inc(s_sum2_p, 1)

            def pair_of_tiles(pair):
                for p in range(2):
                    tile = 2 * pair + p
                    for s in range(STEPS):
                        if s == SUM2_V and live(tile - 1):
                            sum_relu2_v(tile - 1, pair - 1 + p, 1 - p)
                        if s == SUM2_P and live(tile - 1):
                            sum_relu2_p(tile - 1, pair - 1 + p, 1 - p)
                        for j in range(J):
                            for u, _, _ in layer1_work(pair, p, s, Z1_LO[j]):
                                if REST[j] == "vector":
                                    take_rest1(nc.vector, u, j).then_inc(s_z1_lo_v, 1)
                            for u, _, _ in layer1_work(pair, p, s, PRODUCT[j]):
                                product1(u, j)
                        for u, _, par in layer1_work(pair, p, s, CUR1_LO):
                            relu_lo(u, par)
                        for u, its_pair, _ in layer1_work(pair, p, s, SUM1):
                            sum_relu1(u, its_pair)
                        if live(tile) and s % WAYS == 0:
                            add_step(tile, p, s)
                        if isinstance(tile, int) and tile == NT - 1 and s == 1:
                            dve.wait_ge(s_sum1, NT)
                            nc.vector.tensor_reduce(
                                out=sums[:, 0].rearrange("p (t b) -> p t b", t=BLOCKS),
                                in_=sum1[:].rearrange("p t (d b) -> p t b d", d=TD), op=ALU.add,
                                axis=AXX).then_inc(s_sums1, 1)

            over_pairs(dve, pair_of_tiles)
            sum_relu2_v(NT - 1, LAST, (NT - 1) % 2)
            last_terms((NT - 1) % 2)
            sum_relu2_p(NT - 1, LAST, (NT - 1) % 2)
            dve.wait_ge(s_y, 1)
            nc.vector.tensor_copy(y_row[:], bank_y[0:1, :]).then_inc(s_y_row, 1)

        @block.tensor
        def _(pe):
            pe.wait_ge(s_ident, 16)
            pe.wait_ge(s_w1_lo, 2)
            pe.wait_ge(s_w2_lo, G // 2)

            def bank_free(tile, p, s, use):
                n = USES.index((p, s, use))
                for back in range(1, len(USES)):
                    p_was, s_was, use_was = USES[n - back]
                    was = tile - p + p_was - (2 if n < back else 0)
                    if isinstance(was, int) and was < -2:
                        return
                    exists = live(was + 2 if use_was == "x_t" else was)
                    if exists and BANK_OF[n - back] == BANK_OF[n]:
                        break
                else:
                    return
                if use_was == "x_t":
                    pe.wait_ge(s_x_rep, was + 3)
                elif s_was % WAYS == 0:
                    pe.wait_ge(s_added_v, UNITS * was + PER_STEP * (s_was // WAYS + 1)
                               - (ED - 1 - use_was))
                else:
                    pe.wait_ge(s_terms, ED * (G * was + s_was // WAYS) + use_was + 1)

            def transposes(tile, p):
                x_t = bank_of(p, X_T, "x_t")
                pe.wait_ge(s_staged, tile + 3)
                bank_free(tile, p, X_T, "x_t")
                for d in range(TD):
                    last = nc.tensor.transpose(x_t[:, P * d:P * (d + 1)],
                                               staged[:, d].rearrange("p q f -> p (q f)"), ident[:])
                last.then_inc(s_x_t, 1)

            def layer1(tile, j):
                z1_lo_ready(pe, tile, j)
                if j == 0 and due(tile):
                    pe.wait_ge(s_sum1, tile)
                if j == J - 1:
                    nc.tensor.matmul(acc1[:], w1_hi[:, j], z1_hi[:, j], start=False,
                                     stop=True).then_inc(s_l1, 1)
                    return
                nc.tensor.matmul(acc1[:], w1_hi[:, j], z1_hi[:, j], start=j == 0, stop=False)
                nc.tensor.matmul(acc1[:], w1_lo[:, j], z1_hi[:, j], start=False, stop=False)
                nc.tensor.matmul(acc1[:], w1_hi[:, j], z1_lo[:, j], start=False,
                                 stop=False).then_inc(s_l1, 1)

            def mix(tile, par, s):
                g, way = divmod(s, WAYS)
                if s == 0:
                    pe.wait_ge(s_cur1_lo, tile + 1)
                for c in range(ED):
                    bank = bank_of(par, s, c)
                    bank_free(tile, par, s, c)
                    d = ED * way + c
                    hi, lo = (x[:, par, P * d:P * (d + 1)] for x in (cur1_hi, cur1_lo))
                    nc.tensor.matmul(bank[:], hi, w2_hi[:, g], start=True, stop=False)
                    nc.tensor.matmul(bank[:], hi, w2_lo[:, g], start=False, stop=False)
                    nc.tensor.matmul(bank[:], lo, w2_hi[:, g], start=False, stop=True).then_inc(
                        s_mixed, 1)

            def pair_of_tiles(pair):
                for p in range(2):
                    tile = 2 * pair + p
                    for s in range(STEPS):
                        if s == X_T and live(tile + 2):
                            transposes(tile, p)
                        for j in range(J):
                            for u, _, _ in layer1_work(pair, p, s, LAYER1[j]):
                                layer1(u, j)
                        if live(tile):
                            mix(tile, p, s)

            over_pairs(pe, pair_of_tiles)

            def turn(t):
                tiles = PER_BLOCK * (t + 1)
                pe.wait_ge(s_sum2_v, tiles)
                pe.wait_ge(s_sum2_p, tiles)
                for n, (part, c) in enumerate((part, c) for part in (sum2_v, sum2_p)
                                              for c in range(ED)):
                    last = nc.tensor.matmul(acc1[:, P * t:P * (t + 1)], part[:, t, c], ident[:],
                                            start=n == 0, stop=n == 2 * ED - 1)
                return last

            pe.wait_ge(s_sum1, NT)
            for t in range(BLOCKS - 1):
                turn(t)
            pe.wait_ge(s_top_in, TOP_IN)
            pe.wait_ge(s_sums1, 1)
            for m in range(H1 // P):
                if m == 0:
                    pe.wait_ge(s_added_v, UNITS * NT - PER_STEP)
                if m == 1:
                    pe.wait_ge(s_terms, ED * (G * NT - 1))
                if m == 3:
                    pe.wait_ge(s_added_v, UNITS * NT)
                cut = slice(m * P, (m + 1) * P)
                nc.tensor.matmul(banks_h1[m][:], w_top1[:, 0, cut], sums[:, 0], start=True,
                                 stop=False)
                nc.tensor.matmul(banks_h1[m][:], w_top1[0:DENSE, 2, cut], dense[:], start=False,
                                 stop=False)
            turn(BLOCKS - 1).then_inc(s_turned, 1)
            pe.wait_ge(s_sums2, 1)
            for m in range(H1 // P):
                nc.tensor.matmul(banks_h1[m][:], w_top1[:, 1, m * P:(m + 1) * P], sums[:, 1],
                                 start=False, stop=True).then_inc(s_h1, 1)
            for k in range(H1 // P):
                pe.wait_ge(s_hid1, k + 1)
                for m in range(H2 // P):
                    last = nc.tensor.matmul(banks_h2[m][:], w_top2[:, k, m * P:(m + 1) * P],
                                            hid1[:, k], start=(k == 0), stop=(k == H1 // P - 1))
                    if k == H1 // P - 1:
                        last.then_inc(s_h2, 1)
            for k in range(H2 // P):
                pe.wait_ge(s_hid2, k + 1)
                last = nc.tensor.matmul(bank_y[0:1, :], w_top3[:, k:k + 1], hid2[:, k],
                                        start=(k == 0), stop=(k == H2 // P - 1))
            last.then_inc(s_y, 1)


def layer1_rows():
    import numpy as np
    forth, back = -np.ones((P, J), np.int64), -np.ones((P, J), np.int64)
    for p in range(P):
        q, i = divmod(p, F)
        for j in range(J):
            k = Q * j + q if j < J - 1 else F // 2
            if j == J - 1 and (q == 3 or i >= F // 2):
                continue
            m = (i + k) % F
            forth[p, j] = i * F + m
            if k:
                back[p, j] = m * F + i
    return forth, back


def kernel(**inputs):
    import numpy as np
    import concourse.bacc as bacc
    from concourse.bass_utils import run_bass_kernel_spmd

    def laid(x):
        return np.ascontiguousarray(x)

    f0 = np.asarray(inputs["L0_rec_filter_0"])[0]
    f1 = np.asarray(inputs["L0_rec_filter_1"])[0]
    with_none = np.concatenate([f0, np.zeros((1, N1), f0.dtype)])
    forth, back = layer1_rows()
    arrays = {
        "ids": laid(np.asarray(inputs["ids"]).reshape(BLOCKS, P, F).transpose(1, 0, 2)),
        "ident": np.eye(P, dtype=np.float32),
        "w1_forth": laid(with_none[forth].reshape(P, J * N1)),
        "w1_back": laid(with_none[back].reshape(P, J * N1)),
        "w2": laid(f1.reshape(F, N1, N2).transpose(1, 0, 2).reshape(P, G, COLS)),
        "dense": laid(np.asarray(inputs["dense_ctx"]).T),
        "b_top1": laid(np.asarray(inputs["b_top1"]).reshape(H1 // P, P).T),
        "b_top2": laid(np.asarray(inputs["b_top2"]).reshape(H2 // P, P).T),
        "w_top1": laid(inputs["W_top1"]),
        "w_top2": laid(inputs["W_top2"]),
        "w_top3": laid(np.asarray(inputs["W_top3"]).reshape(H2 // P, P).T),
    }
    for f in range(F):
        arrays[f"tbl_{f}"] = laid(inputs[f"tbl_{f}"])
    nc = bacc.Bacc("TRN2", target_bir_lowering=False, num_devices=1)
    aps = {k: nc.dram_tensor(f"in_{k}", x.shape, mybir.dt.from_np(x.dtype),
                             kind="ExternalInput").ap() for k, x in arrays.items()}
    out = nc.dram_tensor("out_y", (1, B), F32, kind="ExternalOutput").ap()
    tower(nc, aps, [aps[f"tbl_{f}"] for f in range(F)], out)
    r = run_bass_kernel_spmd(nc, [{f"in_{k}": x for k, x in arrays.items()}], core_ids=[0])
    return r.results[0]["out_y"].reshape(B, 1)
```
